# Optimizing a Trainium2 kernel written in Bass

```python
import numpy as np
import jax
import jax.numpy as jnp

def _softmax(x, axis=-1):
    return jax.nn.softmax(x, axis=axis)

def _gelu(x):
    return jax.nn.gelu(x, approximate=True)

def _silu(x):
    return jax.nn.silu(x)

def _sigmoid(x):
    return jax.nn.sigmoid(x)

def _layernorm(x, axis=-1, eps=1e-05):
    m = jnp.mean(x, axis=axis, keepdims=True)
    v = jnp.var(x, axis=axis, keepdims=True)
    return (x - m) / jnp.sqrt(v + eps)

def _scatter_add(tgt, idx, src, axis=0):
    return tgt.at[idx].add(src)

def _segment_sum(src, seg, n):
    return jax.ops.segment_sum(src, seg, n)
kernel_name = 'mk_adj_resnorm_d2_adj_r2_c0c3eb'

def setup_inputs(seed: int=0):
    np.random.seed(seed)
    _w = jnp.asarray

    def _rec_inputs():
        import jax
        import jax.numpy as jnp
        _gk = jax.random.key(seed)
        x = -8.776e-05 + 1 * jax.random.normal(jax.random.fold_in(_gk, 1), (4096, 128), jnp.float32)
        _a = jax.random.bernoulli(jax.random.fold_in(_gk, 2), 0.000976562, (4096, 4096))
        _a = jnp.logical_or(_a, jnp.eye(4096, dtype=bool))
        _af = _a.astype(jnp.float32)
        _af = _af * jax.random.uniform(jax.random.fold_in(_gk, 3), (4096, 4096), jnp.float32, 0.05, 1)
        adj = _af
        return (x, adj)
    x, adj = _rec_inputs()

    def _L0_gnn_setup():
        import jax, jax.numpy as jnp
        import numpy as np
        N = 10000
        D = 128
        F = 128
        K = F // 8
        key = jax.random.key(seed)
        k1, k2, k3, k4, k5 = jax.random.split(key, 5)
        h = jax.random.normal(k1, (N, D), dtype=jnp.float32)
        adj = jax.random.uniform(k2, (N, N), dtype=jnp.float32)
        W1 = jax.random.normal(k3, (D, K), dtype=jnp.float32) * 0.05
        W2 = jax.random.normal(k4, (K, D, F), dtype=jnp.float32) * 0.05
        b = jax.random.normal(k5, (K, F), dtype=jnp.float32) * 0.05
        return {'h': h, 'adj': adj, 'W1': W1, 'W2': W2, 'b': b}
    _L0_gnn_all = _L0_gnn_setup()
    _L0_gnn_in = {k: v for k, v in _L0_gnn_all.items() if k in ('W1', 'W2', 'b')}
    del _L0_gnn_all

    def _L1_gnn_setup():
        import jax, jax.numpy as jnp
        import numpy as np
        N = 4096
        D = 128
        CUTOFF = 1.0
        MU = 1.0
        SIGMA = 0.5

        def sensitivity(r, mu, sigma):
            return jnp.exp(-(1.0 / r - 1.0 / mu) ** 2 / (2.0 * sigma * sigma))
        key = jax.random.key(seed)
        k_z, k_d, k_w = jax.random.split(key, 3)
        z = jax.random.normal(k_z, (N, D), dtype=jnp.float32)
        dist_matrix = jax.random.uniform(k_d, (N, N), dtype=jnp.float32) * 2.0 + 0.05
        W = jax.random.normal(k_w, (D, D), dtype=jnp.float32)
        B = jnp.zeros((D,), dtype=jnp.float32)
        return {'z': z, 'dist_matrix': dist_matrix, 'W': W, 'B': B}
    _L1_gnn_all = _L1_gnn_setup()
    _L1_gnn_in = {k: v for k, v in _L1_gnn_all.items() if k in ('W', 'B')}
    del _L1_gnn_all
    return {'x': x, 'adj': adj, 'L0_gnn_W1': _L0_gnn_in['W1'], 'L0_gnn_W2': _L0_gnn_in['W2'], 'L0_gnn_b': _L0_gnn_in['b'], 'L1_gnn_W': _L1_gnn_in['W'], 'L1_gnn_B': _L1_gnn_in['B']}

def reference(x, adj, L0_gnn_W1, L0_gnn_W2, L0_gnn_b, L1_gnn_W, L1_gnn_B):
    import jax
    import jax.numpy as jnp

    def _L0_gnn_ref(h, adj, W1, W2, b):
        import jax, jax.numpy as jnp
        import numpy as np
        N = 10000
        D = 128
        F = 128
        K = F // 8
        node = h @ W1
        hw = jnp.einsum('nc,kcf->nkf', h, W2)
        x = jnp.einsum('nk,nkf->nf', node, hw)
        x = adj @ x
        x = x + node @ b
        return jax.nn.relu(x)

    def _L1_gnn_ref(z, dist_matrix, W, B):
        import jax, jax.numpy as jnp
        import numpy as np
        N = 4096
        D = 128
        CUTOFF = 1.0
        MU = 1.0
        SIGMA = 0.5

        def sensitivity(r, mu, sigma):
            return jnp.exp(-(1.0 / r - 1.0 / mu) ** 2 / (2.0 * sigma * sigma))
        msg = z @ W + B
        sens = sensitivity(dist_matrix, MU, SIGMA)
        weights = jnp.where(dist_matrix < CUTOFF, sens, 0.0)
        return weights @ msg
    x = _layernorm(x + _L0_gnn_ref(x, adj, L0_gnn_W1, L0_gnn_W2, L0_gnn_b), axis=-1)
    x = _layernorm(x + _L1_gnn_ref(x, adj, L1_gnn_W, L1_gnn_B), axis=-1)
    return x

_drawn_inputs = setup_inputs


def setup_inputs(seed=0):
    import zlib

    import numpy as np

    out = dict(_drawn_inputs(seed))
    spreads = {'L1_gnn_B': (0.0, 0.592)}
    factors = {}
    for name, (base, spread) in spreads.items():
        noise = np.random.default_rng([zlib.crc32(name.encode()), seed]).standard_normal(out[name].shape)
        drawn = base * np.exp(spread * noise) if base else spread * noise
        out[name] = jnp.asarray(drawn.astype(out[name].dtype))
    for name, factor in factors.items():
        out[name] = (out[name] * factor).astype(out[name].dtype)
    return out
```

```python
from contextlib import ExitStack

import concourse.bass as bass
from concourse import mybir

F32 = mybir.dt.float32
F32R = mybir.dt.float32r
ALU = mybir.AluOpType
ACT = mybir.ActivationFunctionType

P = 128
CH = 4
BW = CH * P
EPS = 1e-5
TINY = 2.0 ** -60
RING = 4
LEAD = 1
LAG = 2
L1_BANKS = 2


def at_least(engine, semaphore, count):
    if not isinstance(count, int) or count > 0:
        engine.wait_ge(semaphore, count)


def block_of(tensor, index):
    return tensor[:, bass.ds(index * BW, BW)]


def gnn_kernel(nc, adjT, xT, W1, W1T, W2, b0, W, B, outT):
    NB = adjT.shape[0]
    K = W1.shape[1]
    D = xT.shape[0]
    N = NB * BW
    KG = CH
    QUARTERS = K // KG
    GROUPS = CH * QUARTERS
    STEPS = CH * K
    assert D == P and xT.shape[1] == N and NB % RING == 0 and NB % 2 == 0

    with ExitStack() as ctx:
        def sb(name, shape, dt=F32, stack=ctx):
            return stack.enter_context(nc.sbuf_tensor(name, shape, dt))

        def psum(name, shape, stack=ctx):
            return stack.enter_context(nc.psum_tensor(name, shape, F32))

        def sem(name):
            return ctx.enter_context(nc.semaphore(name))

        x0_hi = sb("x0_hi", [P, NB * CH, P], F32R)
        x0_lo = sb("x0_lo", [P, NB * CH, P], F32R)
        sumT = sb("sumT", [P, N])
        row_in = sb("row_in", [P, RING, CH, BW])
        col_in = sb("col_in", [P, RING, CH, BW])
        wts = sb("wts", [P, RING, CH, BW])
        x_row = sb("x_row", [P, BW])
        W_sb = sb("W_sb", [P, P])
        W1_sb = sb("W1_sb", [P, K])
        W1T_sb = sb("W1T_sb", [K, P])
        b0_sb = sb("b0_sb", [K, P])
        W1b = sb("W1b", [P, P])
        B_sb = sb("B_sb", [P, CH, P])
        mean_w = sb("mean_w", [P, P])
        node = sb("node", [P, 2, CH, K])
        with ExitStack() as first:
            W2_in = sb("W2_in", [P, K, P], F32, first)
            W2_hi = sb("W2_hi", [P, K, P], F32R, first)
            W2_lo = sb("W2_lo", [P, K, P], F32R, first)
            x_in = sb("x_in", [P, 2, BW], F32, first)
            x_hi = sb("x_hi", [P, 2, BW], F32R, first)
            x_lo = sb("x_lo", [P, 2, BW], F32R, first)
            x0_acc = sb("x0_acc", [P, 2, CH, P], F32, first)
        adj_hi = sb("adj_hi", [P, 2, CH, BW], F32R)
        adj_lo = sb("adj_lo", [P, 2, CH, BW], F32R)
        y = sb("y", [P, BW])
        yc = sb("yc", [P, BW])
        sq = sb("sq", [P, BW])
        rstd = sb("rstd", [P, BW])
        x1T = sb("x1T", [P, BW])
        msg = sb("msg", [P, CH, P])
        sq_f = [row_in[:, s, 0, :] for s in range(2)]
        rstd_f = [row_in[:, s, 1, :] for s in range(2)]

        acc_ps = psum("acc_ps", [P, BW])
        l1_ps = psum("l1_ps", [P, L1_BANKS, BW])
        node_ps = [l1_ps[:, s, 0:CH * K] for s in range(2)]
        mean_ps = psum("mean_ps", [P, BW])
        with ExitStack() as first:
            hw_ps = psum("hw_ps", [P, 4, KG, P], first)
        var_ps = psum("var_ps", [P, BW])
        msg_ps = psum("msg_ps", [P, CH, P])
        mean_f = [mean_ps[:, :], msg_ps[:, :, :].rearrange("p c f -> p (c f)")]
        var_f = [var_ps[:, :], acc_ps[:, :]]

        const_in = sem("const_in")
        x_in_sem = [sem(f"x_in_{s}") for s in range(2)]
        x_row_in = sem("x_row_in")
        row_tile_in = [sem(f"row_tile_in_{s}") for s in range(RING)]
        col_tile_in = [sem(f"col_tile_in_{s}") for s in range(RING)]
        filled = sem("filled")
        w1b_made = sem("w1b_made")
        w1b_copied = sem("w1b_copied")
        w2_hi_made = sem("w2_hi_made")
        w2_lo_made = sem("w2_lo_made")
        x_hi_made = sem("x_hi_made")
        x_lo_made = sem("x_lo_made")
        node_made = sem("node_made")
        node_copied = sem("node_copied")
        hw_made = sem("hw_made")
        sum_step = sem("sum_step")
        x0_hi_made = sem("x0_hi_made")
        x0_lo_made = sem("x0_lo_made")
        adj_hi_made = [sem(f"adj_hi_made_{s}") for s in range(2)]
        adj_lo_made = sem("adj_lo_made")
        row_tile_done = sem("row_tile_done")
        acc_done = sem("acc_done")
        y_made = sem("y_made")
        mean_made = sem("mean_made")
        yc_made = sem("yc_made")
        sq_made = sem("sq_made")
        var_made = sem("var_made")
        ln_var_made = sem("ln_var_made")
        rstd_made = sem("rstd_made")
        x1_made = sem("x1_made")
        x1_added = sem("x1_added")
        msg_made = sem("msg_made")
        msg_copied = sem("msg_copied")
        ln_made = sem("ln_made")
        inv_made = sem("inv_made")
        square_made = sem("square_made")
        exp_made = sem("exp_made")
        wts_made = sem("wts_made")
        col_tile_done = sem("col_tile_done")
        sum_added = sem("sum_added")
        out_made = sem("out_made")
        out_stored = sem("out_stored")

        CONSTS = 6 * 16

        def row_tile_count(r, g):
            return 16 * (NB // RING * r + g // RING + 1)

        def made_tile(c, u):
            return NB * c + u, u % RING, u % NB, c + u // NB

        block = ctx.enter_context(nc.Block())

        @block.sync
        def _(sp):
            def load_row_tile(r, g):
                at_least(sp, adj_lo_made, NB * r + g - RING + 1)
                sp.dma_start(row_in[:, g % RING, :, :], adjT[r, g]).then_inc(row_tile_in[g % RING], 16)

            def load_col_tile(c, u):
                t, slot, j, col = made_tile(c, u)
                sp.wait_ge(wts_made, t + 1)
                sp.dma_start(col_in[:, slot, :, :], adjT[j, col]).then_inc(col_tile_in[slot], 16)

            def load_x_row(r):
                at_least(sp, y_made, r)
                sp.dma_start(x_row[:, :], block_of(xT, r)).then_inc(x_row_in, 16)

            for g in range(2):
                sp.dma_start(x_in[:, g, :], block_of(xT, g)).then_inc(x_in_sem[g], 16)
            sp.dma_start(W1_sb[:, :], W1).then_inc(const_in, 16)
            sp.dma_start(W2_in[:, :, :], W2.rearrange("k c f -> c k f")).then_inc(const_in, 16)
            sp.dma_start(W1T_sb[:, :], W1T).then_inc(const_in, 16)
            sp.dma_start(b0_sb[:, :], b0).then_inc(const_in, 16)
            sp.dma_start(W_sb[:, :], W).then_inc(const_in, 16)
            sp.dma_start(B_sb[:, :, :], B).then_inc(const_in, 16)
            load_x_row(0)
            for g in range(RING):
                load_row_tile(0, g)
            for u in range(LEAD):
                load_col_tile(0, u)
            with sp.Fori(1, NB // 2) as pair:
                for s in range(2):
                    sp.wait_ge(x_lo_made, pair * 2 + s - 1)
                    sp.wait_ge(node_made, pair * 2 + s - 1)
                    sp.dma_start(x_in[:, s, :], block_of(xT, pair * 2 + s)).then_inc(x_in_sem[s], 16)
            for g in range(RING, NB):
                load_row_tile(0, g)
            with sp.Fori(1, NB) as r:
                load_x_row(r)
                for g in range(NB):
                    load_row_tile(r, g)
                    load_col_tile(r - 1, g + LEAD)
            for u in range(LEAD, NB):
                load_col_tile(NB - 1, u)
            for j in range(NB):
                sp.wait_ge(out_made, j + 1)
                sp.dma_start(block_of(outT, j), block_of(sumT, j)).then_inc(out_stored, 16)
            sp.wait_ge(out_stored, 16 * NB)

        @block.tensor
        def _(pe):
            def first_stage(pair, s):
                g = pair * 2 + s
                pe.wait_ge(x_in_sem[s], 16 * (pair + 1))
                at_least(pe, node_copied, g - 1)
                for c in range(CH):
                    mm = pe.matmul(node_ps[s][:, c * K:(c + 1) * K], x_in[:, s, c * P:(c + 1) * P], W1_sb[:, :],
                                   start=True, stop=True)
                mm.then_inc(node_made, 1)
                pe.wait_ge(x_lo_made, g + 1)
                for n in range(GROUPS):
                    half, q, c2 = n // (2 * QUARTERS), n // 2 % QUARTERS, n % 2
                    c = 2 * half + c2
                    at_least(pe, sum_step, g * STEPS + 2 * KG * ((n - 4) // 2 + 1))
                    out = hw_ps[:, n % 4, :, :]
                    nodes = slice(c * P, (c + 1) * P)
                    ks = slice(q * KG, (q + 1) * KG)
                    pe.matmul(out, x_hi[:, s, nodes], W2_hi[:, ks, :], start=True, stop=False)
                    pe.matmul(out, x_hi[:, s, nodes], W2_lo[:, ks, :], start=False, stop=False)
                    pe.matmul(out, x_lo[:, s, nodes], W2_hi[:, ks, :], start=False, stop=True).then_inc(hw_made, 1)

            def row_tile(r, g):
                if g == 0:
                    at_least(pe, y_made, r)
                pe.wait_ge(adj_lo_made, NB * r + g + 1)
                for c in range(CH):
                    k, s = g * CH + c, g % 2
                    pe.matmul(acc_ps[:, :], x0_hi[:, k, :], adj_hi[:, s, c, :], start=(g == 0 and c == 0), stop=False)
                    pe.matmul(acc_ps[:, :], x0_lo[:, k, :], adj_hi[:, s, c, :], start=False, stop=False)
                    mm = pe.matmul(acc_ps[:, :], x0_hi[:, k, :], adj_lo[:, s, c, :], start=False, stop=False)
                mm.then_inc(row_tile_done, 1)

            def node_bias(r):
                pe.wait_ge(x_row_in, 16 * (r + 1))
                pe.matmul(acc_ps[:, :], W1b[:, :], x_row[:, :], start=False, stop=True).then_inc(acc_done, 1)

            def mean(r):
                pe.wait_ge(y_made, r + 1)
                pe.matmul(mean_ps[:, :], mean_w[:, :], y[:, :], start=True, stop=True).then_inc(mean_made, 1)

            def variance(r):
                pe.wait_ge(sq_made, r + 1)
                pe.matmul(var_ps[:, :], mean_w[:, :], sq[:, :], start=True, stop=True).then_inc(var_made, 1)

            def messages(r):
                pe.wait_ge(x1_made, r + 1)
                for c in range(CH):
                    mm = pe.matmul(msg_ps[:, c, :], x1T[:, c * P:(c + 1) * P], W_sb[:, :], start=True, stop=True)
                mm.then_inc(msg_made, 1)

            def col_tile(c, j):
                t, slot, _, _ = made_tile(c, j)
                if j == 0:
                    pe.wait_ge(msg_copied, c + 1)
                if j >= L1_BANKS:
                    pe.wait_ge(sum_added, t - L1_BANKS + 1)
                pe.wait_ge(wts_made, RING + t + 1)
                for k in range(CH):
                    mm = pe.matmul(l1_ps[:, j % L1_BANKS, :], msg[:, k, :], wts[:, slot, k, :],
                                   start=(k == 0), stop=(k == CH - 1))
                mm.then_inc(col_tile_done, 1)

            pe.sem_inc(col_tile_done, RING)
            pe.wait_ge(const_in, CONSTS)
            pe.matmul(acc_ps[:, 0:P], W1T_sb[:, :], b0_sb[:, :], start=True, stop=True).then_inc(w1b_made, 1)
            pe.wait_ge(w2_lo_made, 1)
            for s in range(2):
                first_stage(0, s)
            with pe.Fori(1, NB // 2) as pair:
                for s in range(2):
                    first_stage(pair, s)

            pe.wait_ge(w1b_copied, 1)
            pe.wait_ge(filled, 2)
            pe.wait_ge(x0_lo_made, NB)
            for g in range(NB):
                row_tile(0, g)
            node_bias(0)
            mean(0)
            with pe.Fori(1, NB) as r:
                for g in range(NB):
                    row_tile(r, g)
                    if g == 0:
                        variance(r - 1)
                    if g == LAG:
                        messages(r - 1)
                    if g >= LAG:
                        col_tile(r - 1, g - LAG)
                node_bias(r)
                for j in range(NB - LAG, NB):
                    col_tile(r - 1, j)
                    if j == NB - LAG:
                        mean(r)
            variance(NB - 1)
            messages(NB - 1)
            for j in range(NB + 2):
                if j < NB:
                    col_tile(NB - 1, j)
                if 1 <= j <= NB:
                    i = j - 1
                    pe.wait_ge(sum_added, NB * (NB - 1) + i + 1)
                    pe.matmul(mean_f[i % 2], mean_w[:, :], block_of(sumT, i),
                              start=True, stop=True).then_inc(mean_made, 1)
                if j >= 2:
                    i = j - 2
                    pe.wait_ge(sq_made, NB + i + 1)
                    pe.matmul(var_f[i % 2], mean_w[:, :], sq_f[i % 2],
                              start=True, stop=True).then_inc(var_made, 1)

        @block.scalar
        def _(act):
            def first_stage(pair, s):
                g = pair * 2 + s
                act.wait_ge(x_in_sem[s], 16 * (pair + 1))
                at_least(act, hw_made, (g - 1) * GROUPS)
                act.activation(x_hi[:, s, :], x_in[:, s, :], ACT.Copy).then_inc(x_hi_made, 1)
                act.wait_ge(node_made, g + 1)
                at_least(act, sum_step, (g - 1) * STEPS)
                act.activation(node[:, s, :, :], node_ps[s].rearrange("p (c k) -> p c k", k=K),
                               ACT.Copy).then_inc(node_copied, 1)

            def round_x0(g, s):
                act.wait_ge(sum_step, (g + 1) * STEPS)
                act.activation(x0_hi[:, bass.ds(g * CH, CH), :], x0_acc[:, s, :, :], ACT.Copy).then_inc(x0_hi_made, 1)

            def take_ln(c, u):
                t, slot, _, _ = made_tile(c, u)
                act.wait_ge(col_tile_in[slot], 16 * (NB // RING * c + u // RING + 1))
                act.wait_ge(col_tile_done, t + 1)
                act.activation(wts[:, slot, :, :], col_in[:, slot, :, :], ACT.Ln, bias=TINY).then_inc(ln_made, 1)

            def take_inverse(c, u):
                t, slot, _, _ = made_tile(c, u)
                act.wait_ge(ln_made, t + 1)
                act.activation(wts[:, slot, :, :], wts[:, slot, :, :], ACT.Exp, scale=-1.0).then_inc(inv_made, 1)

            def take_exp(c, u):
                t, slot, _, _ = made_tile(c, u)
                act.wait_ge(square_made, t + 1)
                act.activation(wts[:, slot, :, :], wts[:, slot, :, :], ACT.Exp, bias=-2.0,
                               scale=-2.0).then_inc(exp_made, 1)

            def make_weights(c, u, new=True, old=True):
                if new:
                    take_ln(c, u)
                if old:
                    take_exp(c, u - 1)
                if new:
                    take_inverse(c, u)

            def round_adj(r, g):
                act.wait_ge(row_tile_in[g % RING], row_tile_count(r, g))
                at_least(act, row_tile_done, NB * r + g - 1)
                act.activation(adj_hi[:, 0, :, :], row_in[:, g % RING, :, :], ACT.Copy).then_inc(adj_hi_made[0], 1)

            def square(n, into, centred):
                act.wait_ge(yc_made, n + 1)
                act.activation(into, centred, ACT.Square).then_inc(sq_made, 1)

            def inverse_root(n, into, variance):
                act.wait_ge(var_made, n + 1)
                act.activation(into, variance, ACT.Ln, bias=EPS).then_inc(ln_var_made, 1)
                act.wait_ge(ln_var_made, n + 1)
                act.activation(into, into, ACT.Exp, scale=-0.5).then_inc(rstd_made, 1)

            act.preload_act_table_set("natural_log_exp_and_others")
            act.wait_ge(const_in, CONSTS)
            act.activation(W2_hi[:, :, :], W2_in[:, :, :], ACT.Copy).then_inc(w2_hi_made, 1)
            for s in range(2):
                first_stage(0, s)
            with act.Fori(1, NB // 2) as pair:
                for s in range(2):
                    round_x0(pair * 2 + (s - 2), s)
                    first_stage(pair, s)
            for s in range(2):
                round_x0(NB - 2 + s, s)

            act.wait_ge(x0_lo_made, NB)
            act.wait_ge(hw_made, NB * GROUPS)
            for g in range(NB):
                if g % 2 == 0:
                    round_adj(0, g)
                if g < LEAD:
                    make_weights(0, g, old=g > 0)
            square(0, sq[:, :], yc[:, :])
            with act.Fori(1, NB) as r:
                for g in range(NB):
                    if g % 2 == 0:
                        round_adj(r, g)
                    make_weights(r - 1, g + LEAD)
                    if g == LAG - 1:
                        inverse_root(r - 1, rstd[:, :], var_ps[:, :])
                square(r, sq[:, :], yc[:, :])
            inverse_root(NB - 1, rstd[:, :], var_ps[:, :])
            for j in range(NB + 2):
                u = j + LEAD
                if u <= NB:
                    make_weights(NB - 1, u, new=u < NB)
                if 1 <= j <= NB:
                    i = j - 1
                    square(NB + i, sq_f[i % 2], block_of(sumT, i))
                if j >= 2:
                    i = j - 2
                    inverse_root(NB + i, rstd_f[i % 2], var_f[i % 2])

        @block.vector
        def _(dve):
            def sum_over_k(g, s):
                dve.wait_ge(node_copied, g + 1)
                at_least(dve, x0_lo_made, g - 1)
                for half in range(CH // 2):
                    for q in range(QUARTERS):
                        n = 2 * (half * QUARTERS + q)
                        dve.wait_ge(hw_made, g * GROUPS + n + 2)
                        for kk in range(KG):
                            for c2 in range(2):
                                c, k = 2 * half + c2, q * KG + kk
                                acc = x0_acc[:, s, c, :]
                                hw = hw_ps[:, (n + c2) % 4, kk, :]
                                scale = node[:, s, c, k:k + 1]
                                done = (n // 2) * 2 * KG + 2 * kk + c2
                                if k == 0:
                                    dve.tensor_scalar(acc, hw, scale, None, ALU.mult).then_inc(sum_step, 1)
                                else:
                                    dve.wait_ge(sum_step, g * STEPS + done - 1)
                                    dve.scalar_tensor_tensor(out=acc, in0=hw, scalar=scale, in1=acc, op0=ALU.mult,
                                                             op1=ALU.add).then_inc(sum_step, 1)

            def mask(c, u):
                t, slot, _, _ = made_tile(c, u)
                dve.wait_ge(exp_made, t + 1)
                dve.scalar_tensor_tensor(out=wts[:, slot, :, :].rearrange("p c n -> p (c n)"),
                                         in0=col_in[:, slot, :, :].rearrange("p c n -> p (c n)"), scalar=1.0,
                                         in1=wts[:, slot, :, :].rearrange("p c n -> p (c n)"), op0=ALU.is_lt,
                                         op1=ALU.mult).then_inc(wts_made, 1)

            def take_square(c, u):
                t, slot, _, _ = made_tile(c, u)
                dve.wait_ge(inv_made, t + 1)
                w = wts[:, slot, :, :].rearrange("p c n -> p (c n)")
                dve.scalar_tensor_tensor(out=w, in0=w, scalar=2.0, in1=w, op0=ALU.subtract,
                                         op1=ALU.mult).then_inc(square_made, 1)

            def make_weights(c, u, new=True, old=True):
                if old:
                    mask(c, u - 1)
                if new:
                    take_square(c, u)

            def round_adj(r, g):
                dve.wait_ge(row_tile_in[g % RING], row_tile_count(r, g))
                at_least(dve, row_tile_done, NB * r + g - 1)
                dve.tensor_copy(adj_hi[:, 1, :, :], row_in[:, g % RING, :, :]).then_inc(adj_hi_made[1], 1)

            def residual(r):
                dve.wait_ge(acc_done, r + 1)
                dve.scalar_tensor_tensor(out=y[:, :], in0=acc_ps[:, :], scalar=0.0, in1=x_row[:, :], op0=ALU.max,
                                         op1=ALU.add).then_inc(y_made, 1)

            def centre(r):
                dve.wait_ge(mean_made, r + 1)
                dve.tensor_tensor(yc[:, :], y[:, :], mean_ps[:, :], ALU.subtract).then_inc(yc_made, 1)

            def scale_row(r):
                dve.wait_ge(rstd_made, r + 1)
                dve.tensor_tensor(x1T[:, :], yc[:, :], rstd[:, :], ALU.mult).then_inc(x1_made, 1)
                dve.wait_ge(x1_made, r + 1)
                at_least(dve, sum_added, r * NB)
                dve.tensor_tensor(block_of(sumT, r), block_of(sumT, r), x1T[:, :], ALU.add).then_inc(x1_added, 1)

            def copy_messages(r):
                dve.wait_ge(msg_made, r + 1)
                dve.tensor_tensor(msg[:, :, :], msg_ps[:, :, :], B_sb[:, :, :], ALU.add).then_inc(msg_copied, 1)

            def add_part(c, j):
                t = made_tile(c, j)[0]
                dve.wait_ge(col_tile_done, RING + t + 1)
                dve.wait_ge(x1_added, c + 1)
                at_least(dve, sum_added, c * NB)
                dve.tensor_tensor(block_of(sumT, j), l1_ps[:, j % L1_BANKS, :], block_of(sumT, j),
                                  ALU.add).then_inc(sum_added, 1)

            dve.sem_inc(wts_made, RING)
            dve.memset(mean_w[:, :], 1.0 / D).then_inc(filled, 1)
            dve.memset(sumT[:, :], 0.0).then_inc(filled, 1)
            dve.wait_ge(w1b_made, 1)
            dve.tensor_copy(W1b[:, :], acc_ps[:, 0:P]).then_inc(w1b_copied, 1)
            for s in range(2):
                sum_over_k(s, s)
            with dve.Fori(1, NB // 2) as pair:
                for s in range(2):
                    sum_over_k(pair * 2 + s, s)

            dve.wait_ge(x0_lo_made, NB)
            dve.wait_ge(filled, 2)
            for g in range(NB):
                if g % 2 == 1:
                    round_adj(0, g)
                if g < LEAD:
                    make_weights(0, g, old=g > 0)
            residual(0)
            centre(0)
            with dve.Fori(1, NB) as r:
                for g in range(NB):
                    if g == LAG:
                        copy_messages(r - 1)
                    if g % 2 == 1:
                        round_adj(r, g)
                    make_weights(r - 1, g + LEAD)
                    if g == LAG - 1:
                        scale_row(r - 1)
                    if g > LAG:
                        add_part(r - 1, g - LAG - 1)
                first = NB - LAG - 1
                residual(r)
                add_part(r - 1, first)
                add_part(r - 1, first + 1)
                centre(r)
                for j in range(first + 2, NB):
                    add_part(r - 1, j)
            scale_row(NB - 1)
            copy_messages(NB - 1)
            for j in range(NB + 2):
                u = j + LEAD
                if u <= NB:
                    make_weights(NB - 1, u, new=u < NB)
                if j < NB:
                    add_part(NB - 1, j)
                if 1 <= j <= NB:
                    i = j - 1
                    dve.wait_ge(mean_made, NB + i + 1)
                    dve.tensor_tensor(block_of(sumT, i), block_of(sumT, i), mean_f[i % 2],
                                      ALU.subtract).then_inc(yc_made, 1)
                if j >= 2:
                    i = j - 2
                    dve.wait_ge(rstd_made, NB + i + 1)
                    dve.tensor_tensor(block_of(sumT, i), block_of(sumT, i), rstd_f[i % 2],
                                      ALU.mult).then_inc(out_made, 1)

        @block.gpsimd
        def _(pool):
            def first_stage(g, s):
                pool.wait_ge(x_hi_made, g + 1)
                pool.tensor_tensor(x_lo[:, s, :], x_in[:, s, :], x_hi[:, s, :], ALU.subtract).then_inc(x_lo_made, 1)

            def split_x0(g, s):
                pool.wait_ge(x0_hi_made, g + 1)
                pool.tensor_tensor(x0_lo[:, bass.ds(g * CH, CH), :], x0_acc[:, s, :, :],
                                   x0_hi[:, bass.ds(g * CH, CH), :], ALU.subtract).then_inc(x0_lo_made, 1)

            def split_adj(r, g):
                s = g % 2
                pool.wait_ge(adj_hi_made[s], NB // 2 * r + g // 2 + 1)
                pool.tensor_tensor(adj_lo[:, s, :, :], row_in[:, g % RING, :, :], adj_hi[:, s, :, :],
                                   ALU.subtract).then_inc(adj_lo_made, 1)

            pool.wait_ge(w2_hi_made, 1)
            pool.tensor_tensor(W2_lo[:, :, :], W2_in[:, :, :], W2_hi[:, :, :], ALU.subtract).then_inc(w2_lo_made, 1)
            for s in range(2):
                first_stage(s, s)
            with pool.Fori(1, NB // 2) as pair:
                for s in range(2):
                    split_x0(pair * 2 + (s - 2), s)
                    first_stage(pair * 2 + s, s)
            for s in range(2):
                split_x0(NB - 2 + s, s)
            for g in range(NB):
                split_adj(0, g)
            with pool.Fori(1, NB) as r:
                for g in range(NB):
                    split_adj(r, g)


def kernel(x, adj, L0_gnn_W1, L0_gnn_W2, L0_gnn_b, L1_gnn_W, L1_gnn_B):
    import numpy as np
    import concourse.bacc as bacc
    from concourse.bass_utils import run_bass_kernel_spmd

    x, adj, W1, W2, b0, W, B = (np.asarray(a) for a in (x, adj, L0_gnn_W1, L0_gnn_W2, L0_gnn_b, L1_gnn_W, L1_gnn_B))
    n, d = x.shape
    blocks = n // BW
    adjT = adj.reshape(blocks, BW, blocks, CH, P).transpose(0, 2, 4, 3, 1)
    arrays = {
        "adjT": adjT, "xT": x.T, "W1": W1, "W1T": W1.T, "W2": W2, "b0": b0, "W": W,
        "B": np.broadcast_to(B, (P, CH, d)),
    }
    arrays = {f"{name}_dram": np.ascontiguousarray(a) for name, a in arrays.items()}
    nc = bacc.Bacc("TRN2", target_bir_lowering=False, num_devices=1)
    args = [nc.dram_tensor(name, a.shape, mybir.dt.from_np(a.dtype), kind="ExternalInput").ap()
            for name, a in arrays.items()]
    outT = nc.dram_tensor("outT_dram", (d, n), F32, kind="ExternalOutput").ap()
    gnn_kernel(nc, *args, outT)
    result = run_bass_kernel_spmd(nc, [arrays], core_ids=[0])
    return np.ascontiguousarray(result.results[0]["outT_dram"].T)
```

```python
from contextlib import ExitStack

import concourse.bass as bass
from concourse import mybir

F32 = mybir.dt.float32
F32R = mybir.dt.float32r
ALU = mybir.AluOpType
ACT = mybir.ActivationFunctionType

P = 128
CH = 4
BW = CH * P
EPS = 1e-5
TINY = 2.0 ** -60
SCALE_STEP = 1
ACT_ROUNDS = (0, 2, 4, 6)
RING = 4
LAG = 3
LEAD = 1
SPLIT_LEAD = 3
ROW_LEAD = 5
COL_LEAD = 3
L1_BANKS = 2


def at_least(engine, semaphore, count):
    if not isinstance(count, int) or count > 0:
        engine.wait_ge(semaphore, count)


def block_of(tensor, index):
    return tensor[:, bass.ds(index * BW, BW)]


def gnn_kernel(nc, adjT, xT, W1, W1T, W2, b0, W, B, outT):
    NB = adjT.shape[0]
    K = W1.shape[1]
    D = xT.shape[0]
    N = NB * BW
    KG = CH
    QUARTERS = K // KG
    HALF = CH // 2
    GROUPS = HALF * QUARTERS
    STEPS = HALF * (K + 1)
    FOLDS = HALF * (K.bit_length() - 1)
    assert D == P and xT.shape[1] == N and NB % RING == 0 and NB % 2 == 0

    with ExitStack() as ctx:
        def sb(name, shape, dt=F32, stack=ctx):
            return stack.enter_context(nc.sbuf_tensor(name, shape, dt))

        def psum(name, shape, stack=ctx):
            return stack.enter_context(nc.psum_tensor(name, shape, F32))

        def sem(name):
            return ctx.enter_context(nc.semaphore(name))

        x0_hi = sb("x0_hi", [P, NB * CH, P], F32R)
        x0_lo = sb("x0_lo", [P, NB * CH, P], F32R)
        sumT = sb("sumT", [P, N])
        row_in = sb("row_in", [P, RING, CH, BW])
        col_in = sb("col_in", [P, RING, CH, BW])
        wts = sb("wts", [P, RING, CH, BW])
        x_row = sb("x_row", [P, BW])
        W_sb = sb("W_sb", [P, P])
        W1_sb = sb("W1_sb", [P, K])
        W1T_sb = sb("W1T_sb", [K, P])
        b0_sb = sb("b0_sb", [K, P])
        W1b = sb("W1b", [P, P])
        B_sb = sb("B_sb", [P, CH, P])
        mean_w = sb("mean_w", [P, P])
        node = sb("node", [P, 2, CH, K])
        with ExitStack() as first:
            W2_hi = sb("W2_hi", [P, K, P], F32R, first)
            W2_lo = sb("W2_lo", [P, K, P], F32R, first)
            x_in = sb("x_in", [P, 2, BW], F32, first)
            x_hi = sb("x_hi", [P, 2, BW], F32R, first)
            x_lo = sb("x_lo", [P, 2, BW], F32R, first)
            x0_acc = sb("x0_acc", [P, 2, CH, P], F32, first)
            part_acc = sb("part_acc", [P, HALF, 2, P], F32, first)
            prods = sb("prods", [P, HALF, K, P], F32, first)
        adj_hi = sb("adj_hi", [P, 2, CH, BW], F32R)
        adj_lo = sb("adj_lo", [P, 2, CH, BW], F32R)
        y = sb("y", [P, BW])
        yc = sb("yc", [P, BW])
        sq = sb("sq", [P, BW])
        rstd = sb("rstd", [P, BW])
        x1T = sb("x1T", [P, BW])
        msg = sb("msg", [P, CH, P])
        W2_in = wts[:, 0, :, :].rearrange("p c (k f) -> p (c k) f", f=P)
        sq_f = [row_in[:, s, 0, :] for s in range(2)]
        rstd_f = [row_in[:, s, 1, :] for s in range(2)]

        acc_ps = psum("acc_ps", [P, BW])
        l1_ps = psum("l1_ps", [P, L1_BANKS, BW])
        node_ps = [l1_ps[:, s, 0:CH * K] for s in range(2)]
        mean_ps = psum("mean_ps", [P, BW])
        with ExitStack() as first:
            hw_ps = psum("hw_ps", [P, 2, 2, KG, P], first)
        var_ps = psum("var_ps", [P, BW])
        msg_ps = psum("msg_ps", [P, CH, P])
        mean_f = [mean_ps[:, :], msg_ps[:, :, :].rearrange("p c f -> p (c f)")]
        var_f = [var_ps[:, :], acc_ps[:, :]]

        const_in = sem("const_in")
        x_in_sem = [sem(f"x_in_{s}") for s in range(2)]
        x_row_in = sem("x_row_in")
        row_tile_in = [sem(f"row_tile_in_{s}") for s in range(RING)]
        col_tile_in = [sem(f"col_tile_in_{s}") for s in range(RING)]
        filled = sem("filled")
        w1b_made = sem("w1b_made")
        w1b_copied = sem("w1b_copied")
        w2_hi_made = sem("w2_hi_made")
        w2_lo_made = sem("w2_lo_made")
        x_hi_made = sem("x_hi_made")
        x_lo_made = sem("x_lo_made")
        node_made = sem("node_made")
        node_copied = sem("node_copied")
        hw_made = [sem(f"hw_made_{h}") for h in range(2)]
        prods_made = sem("prods_made")
        fold_step = sem("fold_step")
        sum_step = sem("sum_step")
        x0_hi_made = sem("x0_hi_made")
        x0_lo_made = sem("x0_lo_made")
        adj_hi_made = [sem(f"adj_hi_made_{s}") for s in range(2)]
        adj_lo_made = [sem(f"adj_lo_made_{s}") for s in range(2)]
        row_tile_done = sem("row_tile_done")
        acc_done = sem("acc_done")
        y_made = sem("y_made")
        mean_made = sem("mean_made")
        yc_made = sem("yc_made")
        sq_made = sem("sq_made")
        var_made = sem("var_made")
        ln_var_made = sem("ln_var_made")
        rstd_made = sem("rstd_made")
        x1_made = sem("x1_made")
        x1_added = sem("x1_added")
        msg_made = sem("msg_made")
        msg_copied = sem("msg_copied")
        ln_made = sem("ln_made")
        inv_made = sem("inv_made")
        square_made = sem("square_made")
        exp_made = sem("exp_made")
        wts_made = sem("wts_made")
        col_tile_done = sem("col_tile_done")
        sum_added = sem("sum_added")
        out_made = sem("out_made")
        out_stored = sem("out_stored")

        CONSTS = 6 * 16

        def row_tile_count(r, g):
            return 16 * (NB // RING * r + g // RING + 1)

        def numbered(c, u):
            return NB * c + u, u % RING, u % NB, c + u // NB

        def exists(r, g):
            return not isinstance(r, int) or 0 <= NB * r + g < NB * NB

        def dve_steps(n):
            return KG * (n + 1) + (n + 1) // QUARTERS

        def lo_count(r, g):
            return NB // 2 * r + g // 2 + 1

        block = ctx.enter_context(nc.Block())

        @block.sync
        def _(sp):
            def load_row_tile(r, g):
                at_least(sp, adj_lo_made[g % 2], lo_count(r, g - RING))
                sp.dma_start(row_in[:, g % RING, :, :], adjT[r + g // NB, g % NB]).then_inc(row_tile_in[g % RING], 16)

            def load_col_tile(c, u):
                t, slot, j, col = numbered(c, u)
                at_least(sp, wts_made, t - RING + 1)
                sp.dma_start(col_in[:, slot, :, :], adjT[j, col]).then_inc(col_tile_in[slot], 16)

            def load_x_row(r):
                at_least(sp, y_made, r)
                sp.dma_start(x_row[:, :], block_of(xT, r)).then_inc(x_row_in, 16)

            def load_x(pair, s):
                g = pair * 2 + s
                at_least(sp, x_lo_made, g - 1)
                at_least(sp, node_made, g - 1)
                sp.dma_start(x_in[:, s, :], block_of(xT, g)).then_inc(x_in_sem[s], 16)

            load_x(0, 0)
            sp.dma_start(W1_sb[:, :], W1).then_inc(const_in, 16)
            sp.dma_start(W2_in, W2.rearrange("k c f -> c k f")).then_inc(const_in, 16)
            load_x(0, 1)
            sp.dma_start(W1T_sb[:, :], W1T).then_inc(const_in, 16)
            sp.dma_start(b0_sb[:, :], b0).then_inc(const_in, 16)
            sp.dma_start(W_sb[:, :], W).then_inc(const_in, 16)
            sp.dma_start(B_sb[:, :, :], B).then_inc(const_in, 16)
            with sp.Fori(1, NB // 2) as pair:
                for s in range(2):
                    load_x(pair, s)
            load_x_row(0)
            for g in range(ROW_LEAD):
                load_row_tile(0, g)

            def loads(r):
                if not isinstance(r, int) or 0 < r < NB:
                    load_x_row(r)
                for g in range(NB):
                    if exists(r, g + ROW_LEAD):
                        load_row_tile(r, g + ROW_LEAD)
                    if exists(r - 1, g + COL_LEAD):
                        load_col_tile(r - 1, g + COL_LEAD)

            for r in (0, 1):
                loads(r)
            with sp.Fori(2, NB - 1) as r:
                loads(r)
            for r in (NB - 1, NB):
                loads(r)
            for j in range(NB):
                sp.wait_ge(out_made, j + 1)
                sp.dma_start(block_of(outT, j), block_of(sumT, j)).then_inc(out_stored, 16)
            sp.wait_ge(out_stored, 16 * NB)

        @block.tensor
        def _(pe):
            def node_product(pair, s):
                g = pair * 2 + s
                pe.wait_ge(x_in_sem[s], 16 * (pair + 1))
                at_least(pe, node_copied, g - 1)
                for c in range(CH):
                    mm = pe.matmul(node_ps[s][:, c * K:(c + 1) * K], x_in[:, s, c * P:(c + 1) * P], W1_sb[:, :],
                                   start=True, stop=True)
                mm.then_inc(node_made, 1)

            def hidden(pair, s):
                g = pair * 2 + s
                pe.wait_ge(x_lo_made, g + 1)
                for n in range(GROUPS):
                    for half in range(2):
                        c = HALF * half + n // QUARTERS
                        q = n % QUARTERS
                        if half == 0:
                            at_least(pe, sum_step, (g - int(n < 2)) * STEPS + dve_steps((n - 2) % GROUPS))
                        else:
                            at_least(pe, prods_made, g * GROUPS + n - 1)
                        out = hw_ps[:, half, n % 2, :, :]
                        nodes = slice(c * P, (c + 1) * P)
                        ks = slice(q * KG, (q + 1) * KG)
                        pe.matmul(out, x_hi[:, s, nodes], W2_hi[:, ks, :], start=True, stop=False)
                        pe.matmul(out, x_hi[:, s, nodes], W2_lo[:, ks, :], start=False, stop=False)
                        pe.matmul(out, x_lo[:, s, nodes], W2_hi[:, ks, :], start=False,
                                  stop=True).then_inc(hw_made[half], 1)

            def first_stage(pair, s):
                if not isinstance(pair, int) or pair * 2 + s + 1 < NB:
                    node_product(pair + s, 1 - s)
                hidden(pair, s)

            def row_tile(r, g):
                if g == 0:
                    at_least(pe, y_made, r)
                pe.wait_ge(adj_lo_made[g % 2], lo_count(r, g))
                for c in range(CH):
                    k, s = g * CH + c, g % 2
                    pe.matmul(acc_ps[:, :], x0_hi[:, k, :], adj_hi[:, s, c, :], start=(g == 0 and c == 0), stop=False)
                    pe.matmul(acc_ps[:, :], x0_lo[:, k, :], adj_hi[:, s, c, :], start=False, stop=False)
                    mm = pe.matmul(acc_ps[:, :], x0_hi[:, k, :], adj_lo[:, s, c, :], start=False, stop=False)
                mm.then_inc(row_tile_done, 1)

            def node_bias(r):
                pe.wait_ge(x_row_in, 16 * (r + 1))
                pe.matmul(acc_ps[:, :], W1b[:, :], x_row[:, :], start=False, stop=True).then_inc(acc_done, 1)

            def mean(r):
                pe.wait_ge(y_made, r + 1)
                pe.matmul(mean_ps[:, :], mean_w[:, :], y[:, :], start=True, stop=True).then_inc(mean_made, 1)

            def variance(r):
                pe.wait_ge(sq_made, r + 1)
                pe.matmul(var_ps[:, :], mean_w[:, :], sq[:, :], start=True, stop=True).then_inc(var_made, 1)

            def messages(r):
                pe.wait_ge(x1_made, r + 1)
                for c in range(CH):
                    mm = pe.matmul(msg_ps[:, c, :], x1T[:, c * P:(c + 1) * P], W_sb[:, :], start=True, stop=True)
                mm.then_inc(msg_made, 1)

            def col_tile(c, u):
                t, slot, j, col = numbered(c, u)
                if j == 0:
                    pe.wait_ge(msg_copied, col + 1)
                at_least(pe, sum_added, t - L1_BANKS + 1)
                pe.wait_ge(wts_made, t + 1)
                for k in range(CH):
                    mm = pe.matmul(l1_ps[:, j % L1_BANKS, :], msg[:, k, :], wts[:, slot, k, :],
                                   start=(k == 0), stop=(k == CH - 1))
                mm.then_inc(col_tile_done, 1)

            def row(r):
                before = not isinstance(r, int) or r > 0
                for g in range(NB):
                    if before and g == LAG:
                        messages(r - 1)
                    if exists(r, g):
                        row_tile(r, g)
                    if exists(r, g) and g == NB - 1:
                        node_bias(r)
                    if before and g == 0:
                        mean(r - 1)
                    if exists(r - 1, g - LAG):
                        col_tile(r - 1, g - LAG)
                    if before and g == 0:
                        variance(r - 1)
                    if isinstance(r, int) and r == NB:
                        last_norms(g - LAG)

            def last_norms(j):
                if 0 <= j - 1 < NB:
                    i = j - 1
                    pe.wait_ge(sum_added, NB * (NB - 1) + i + 1)
                    pe.matmul(mean_f[i % 2], mean_w[:, :], block_of(sumT, i),
                              start=True, stop=True).then_inc(mean_made, 1)
                if 0 <= j - 2 < NB:
                    i = j - 2
                    pe.wait_ge(sq_made, NB + i + 1)
                    pe.matmul(var_f[i % 2], mean_w[:, :], sq_f[i % 2],
                              start=True, stop=True).then_inc(var_made, 1)

            pe.wait_ge(const_in, CONSTS)
            pe.matmul(acc_ps[:, 0:P], W1T_sb[:, :], b0_sb[:, :], start=True, stop=True).then_inc(w1b_made, 1)
            pe.wait_ge(w2_lo_made, 1)
            node_product(0, 0)
            for s in range(2):
                first_stage(0, s)
            with pe.Fori(1, NB // 2 - 1) as pair:
                for s in range(2):
                    first_stage(pair, s)
            for s in range(2):
                first_stage(NB // 2 - 1, s)

            pe.wait_ge(w1b_copied, 1)
            pe.wait_ge(filled, 2)
            pe.wait_ge(x0_lo_made, NB)
            for r in (0, 1):
                row(r)
            with pe.Fori(2, NB - 1) as r:
                row(r)
            for r in (NB - 1, NB):
                row(r)
            for j in range(NB - LAG, NB):
                col_tile(NB - 1, j)
                last_norms(j)
            for j in range(NB, NB + 2):
                last_norms(j)

        @block.scalar
        def _(act):
            def copy_node(g, s):
                act.wait_ge(node_made, g + 1)
                at_least(act, sum_step, (g - 1) * STEPS)
                at_least(act, prods_made, (g - 1) * GROUPS)
                act.activation(node[:, s, :, :], node_ps[s].rearrange("p (c k) -> p c k", k=K),
                               ACT.Copy).then_inc(node_copied, 1)

            def first_stage(pair, s):
                g = pair * 2 + s
                if not isinstance(pair, int) or g + 1 < NB:
                    copy_node(g + 1, 1 - s)
                act.wait_ge(node_copied, g + 1)
                for n in range(GROUPS):
                    c2, q = n // QUARTERS, n % QUARTERS
                    act.wait_ge(hw_made[1], g * GROUPS + n + 1)
                    if q == 0:
                        at_least(act, fold_step, (g - 1) * FOLDS + (c2 + 1) * FOLDS // HALF)
                    for kk in range(KG):
                        k = q * KG + kk
                        op = act.activation(prods[:, c2, k, :], hw_ps[:, 1, n % 2, kk, :], ACT.Copy,
                                            scale=node[:, s, HALF + c2, k:k + 1])
                    op.then_inc(prods_made, 1)

            def take_ln(c, u):
                t, slot, _, _ = numbered(c, u)
                act.wait_ge(col_tile_in[slot], 16 * (NB // RING * c + u // RING + 1))
                at_least(act, col_tile_done, t - RING + 1)
                act.activation(wts[:, slot, :, :], col_in[:, slot, :, :], ACT.Ln, bias=TINY).then_inc(ln_made, 1)

            def take_inverse(c, u):
                t, slot, _, _ = numbered(c, u)
                act.wait_ge(ln_made, t + 1)
                act.activation(wts[:, slot, :, :], wts[:, slot, :, :], ACT.Exp, scale=-1.0).then_inc(inv_made, 1)

            def take_exp(c, u):
                t, slot, _, _ = numbered(c, u)
                act.wait_ge(square_made, t + 1)
                act.activation(wts[:, slot, :, :], wts[:, slot, :, :], ACT.Exp, bias=-2.0,
                               scale=-2.0).then_inc(exp_made, 1)

            def make_weights(c, u):
                if exists(c, u):
                    take_ln(c, u)
                    take_inverse(c, u)
                if exists(c, u - 1):
                    take_exp(c, u - 1)

            def round_adj(r, g):
                act.wait_ge(row_tile_in[g % RING], row_tile_count(r, g))
                at_least(act, row_tile_done, NB * r + g - 1)
                act.activation(adj_hi[:, g % 2, :, :], row_in[:, g % RING, :, :],
                               ACT.Copy).then_inc(adj_hi_made[g % 2], 1)

            def square(n, into, centred):
                act.wait_ge(yc_made, n + 1)
                act.activation(into, centred, ACT.Square).then_inc(sq_made, 1)

            def inverse_root(n, into, variance):
                act.wait_ge(var_made, n + 1)
                act.activation(into, variance, ACT.Ln, bias=EPS).then_inc(ln_var_made, 1)
                act.wait_ge(ln_var_made, n + 1)
                act.activation(into, into, ACT.Exp, scale=-0.5).then_inc(rstd_made, 1)

            act.preload_act_table_set("natural_log_exp_and_others")
            act.wait_ge(const_in, CONSTS)
            act.activation(W2_hi[:, :, :], W2_in, ACT.Copy).then_inc(w2_hi_made, 1)
            copy_node(0, 0)
            for s in range(2):
                first_stage(0, s)
            with act.Fori(1, NB // 2 - 1) as pair:
                for s in range(2):
                    first_stage(pair, s)
            for s in range(2):
                first_stage(NB // 2 - 1, s)

            act.wait_ge(x0_lo_made, NB)
            act.wait_ge(hw_made[0], NB * GROUPS)
            for g in range(SPLIT_LEAD):
                if g in ACT_ROUNDS:
                    round_adj(0, g)

            def row(r):
                before = not isinstance(r, int) or r > 0
                for g in range(NB):
                    make_weights(r - 1, g + LEAD)
                    if exists(r, g + SPLIT_LEAD) and (g + SPLIT_LEAD) % NB in ACT_ROUNDS:
                        round_adj(r, g + SPLIT_LEAD)
                    if exists(r, g) and g == NB - 1:
                        square(r, sq[:, :], yc[:, :])
                    if before and g == 0:
                        inverse_root(r - 1, rstd[:, :], var_ps[:, :])
                    if isinstance(r, int) and r == NB:
                        last_norms(g - LAG)

            def last_norms(j):
                if 0 <= j - 1 < NB:
                    i = j - 1
                    square(NB + i, sq_f[i % 2], block_of(sumT, i))
                if 0 <= j - 2 < NB:
                    i = j - 2
                    inverse_root(NB + i, rstd_f[i % 2], var_f[i % 2])

            for r in (0, 1):
                row(r)
            with act.Fori(2, NB - 1) as r:
                row(r)
            for r in (NB - 1, NB):
                row(r)
            for j in range(NB - LAG, NB + 2):
                last_norms(j)

        @block.vector
        def _(dve):
            def round_x(pair, s):
                g = pair * 2 + s
                dve.wait_ge(x_in_sem[s], 16 * (pair + 1))
                for half in range(2):
                    at_least(dve, hw_made[half], (g - 1) * GROUPS)
                dve.tensor_copy(x_hi[:, s, :], x_in[:, s, :]).then_inc(x_hi_made, 1)

            def sum_over_k(g, s):
                dve.wait_ge(node_copied, g + 1)
                at_least(dve, x0_lo_made, g - 1)
                for n in range(GROUPS):
                    c, q = n // QUARTERS, n % QUARTERS
                    dve.wait_ge(hw_made[0], g * GROUPS + n + 1)
                    for kk in range(KG):
                        k = q * KG + kk
                        acc = part_acc[:, c, k % 2, :]
                        hw = hw_ps[:, 0, n % 2, kk, :]
                        scale = node[:, s, c, k:k + 1]
                        step = g * STEPS + c * (K + 1) + k
                        if k < 2:
                            dve.tensor_scalar(acc, hw, scale, None, ALU.mult).then_inc(sum_step, 1)
                        else:
                            dve.wait_ge(sum_step, step - 1)
                            dve.scalar_tensor_tensor(out=acc, in0=hw, scalar=scale, in1=acc, op0=ALU.mult,
                                                     op1=ALU.add).then_inc(sum_step, 1)
                    if q == QUARTERS - 1:
                        dve.wait_ge(sum_step, g * STEPS + c * (K + 1) + K)
                        dve.tensor_tensor(x0_acc[:, s, c, :], part_acc[:, c, 0, :], part_acc[:, c, 1, :],
                                          ALU.add).then_inc(sum_step, 1)

            def round_x0(g, s):
                dve.wait_ge(sum_step, (g + 1) * STEPS)
                dve.wait_ge(fold_step, (g + 1) * FOLDS)
                dve.tensor_copy(x0_hi[:, bass.ds(g * CH, CH), :], x0_acc[:, s, :, :]).then_inc(x0_hi_made, 1)

            def first_stage(pair, s):
                g = pair * 2 + s
                if not isinstance(pair, int) or g + 1 < NB:
                    round_x(pair + s, 1 - s)
                sum_over_k(g, s)
                if not isinstance(pair, int) or g > 0:
                    round_x0(g - 1, 1 - s)

            def mask(c, u):
                t, slot, _, _ = numbered(c, u)
                dve.wait_ge(exp_made, t + 1)
                dve.scalar_tensor_tensor(out=wts[:, slot, :, :].rearrange("p c n -> p (c n)"),
                                         in0=col_in[:, slot, :, :].rearrange("p c n -> p (c n)"), scalar=1.0,
                                         in1=wts[:, slot, :, :].rearrange("p c n -> p (c n)"), op0=ALU.is_lt,
                                         op1=ALU.mult).then_inc(wts_made, 1)

            def take_square(c, u):
                t, slot, _, _ = numbered(c, u)
                dve.wait_ge(inv_made, t + 1)
                w = wts[:, slot, :, :].rearrange("p c n -> p (c n)")
                dve.scalar_tensor_tensor(out=w, in0=w, scalar=2.0, in1=w, op0=ALU.subtract,
                                         op1=ALU.mult).then_inc(square_made, 1)

            def make_weights(c, u):
                if exists(c, u - 1):
                    mask(c, u - 1)
                if exists(c, u):
                    take_square(c, u)

            def round_adj(r, g):
                dve.wait_ge(row_tile_in[g % RING], row_tile_count(r, g))
                at_least(dve, row_tile_done, NB * r + g - 1)
                dve.tensor_copy(adj_hi[:, g % 2, :, :], row_in[:, g % RING, :, :]).then_inc(adj_hi_made[g % 2], 1)

            def split_adj(r, g):
                dve.wait_ge(adj_hi_made[g % 2], lo_count(r, g))
                dve.tensor_tensor(adj_lo[:, g % 2, :, :], row_in[:, g % RING, :, :], adj_hi[:, g % 2, :, :],
                                  ALU.subtract).then_inc(adj_lo_made[g % 2], 1)

            def residual(r):
                dve.wait_ge(acc_done, r + 1)
                dve.scalar_tensor_tensor(out=y[:, :], in0=acc_ps[:, :], scalar=0.0, in1=x_row[:, :], op0=ALU.max,
                                         op1=ALU.add).then_inc(y_made, 1)

            def centre(r):
                dve.wait_ge(mean_made, r + 1)
                dve.tensor_tensor(yc[:, :], y[:, :], mean_ps[:, :], ALU.subtract).then_inc(yc_made, 1)

            def scale_row(r):
                dve.wait_ge(rstd_made, r + 1)
                dve.tensor_tensor(x1T[:, :], yc[:, :], rstd[:, :], ALU.mult).then_inc(x1_made, 1)
                dve.wait_ge(x1_made, r + 1)
                at_least(dve, sum_added, r * NB + SCALE_STEP - LAG)
                dve.tensor_tensor(block_of(sumT, r), block_of(sumT, r), x1T[:, :], ALU.add).then_inc(x1_added, 1)

            def copy_messages(r):
                dve.wait_ge(msg_made, r + 1)
                dve.tensor_tensor(msg[:, :, :], msg_ps[:, :, :], B_sb[:, :, :], ALU.add).then_inc(msg_copied, 1)

            def add_part(c, u):
                t, _, j, col = numbered(c, u)
                dve.wait_ge(col_tile_done, t + 1)
                at_least(dve, x1_added, c + int(u + LAG >= SCALE_STEP))
                at_least(dve, sum_added, col * NB)
                dve.tensor_tensor(block_of(sumT, j), l1_ps[:, j % L1_BANKS, :], block_of(sumT, j),
                                  ALU.add).then_inc(sum_added, 1)

            dve.memset(mean_w[:, :], 1.0 / D).then_inc(filled, 1)
            dve.memset(sumT[:, :], 0.0).then_inc(filled, 1)
            dve.wait_ge(w1b_made, 1)
            dve.tensor_copy(W1b[:, :], acc_ps[:, 0:P]).then_inc(w1b_copied, 1)
            round_x(0, 0)
            for s in range(2):
                first_stage(0, s)
            with dve.Fori(1, NB // 2 - 1) as pair:
                for s in range(2):
                    first_stage(pair, s)
            for s in range(2):
                first_stage(NB // 2 - 1, s)
            round_x0(NB - 1, 1)

            dve.wait_ge(x0_lo_made, NB)
            dve.wait_ge(filled, 2)
            for g in range(SPLIT_LEAD):
                if g not in ACT_ROUNDS:
                    round_adj(0, g)
                    split_adj(0, g)

            def row(r):
                before = not isinstance(r, int) or r > 0
                for g in range(NB):
                    if exists(r, g) and g == NB - 2:
                        residual(r)
                    if exists(r, g) and g == NB - 1:
                        centre(r)
                    if exists(r, g + SPLIT_LEAD) and (g + SPLIT_LEAD) % NB not in ACT_ROUNDS:
                        round_adj(r, g + SPLIT_LEAD)
                        if isinstance(r, int) and r == 0 and g + SPLIT_LEAD < NB:
                            split_adj(r, g + SPLIT_LEAD)
                    if before and g == SCALE_STEP:
                        scale_row(r - 1)
                    if before and g == LAG - 1:
                        copy_messages(r - 1)
                    if exists(r - 1, g - LAG):
                        add_part(r - 1, g - LAG)
                    make_weights(r - 1, g + LEAD)
                    if isinstance(r, int) and r == NB:
                        last_norms(g - LAG)

            def last_norms(j):
                if 0 <= j - 1 < NB:
                    i = j - 1
                    dve.wait_ge(mean_made, NB + i + 1)
                    dve.tensor_tensor(block_of(sumT, i), block_of(sumT, i), mean_f[i % 2],
                                      ALU.subtract).then_inc(yc_made, 1)
                if 0 <= j - 2 < NB:
                    i = j - 2
                    dve.wait_ge(rstd_made, NB + i + 1)
                    dve.tensor_tensor(block_of(sumT, i), block_of(sumT, i), rstd_f[i % 2],
                                      ALU.mult).then_inc(out_made, 1)

            for r in (0, 1):
                row(r)
            with dve.Fori(2, NB - 1) as r:
                row(r)
            for r in (NB - 1, NB):
                row(r)
            for j in range(NB - LAG, NB + 2):
                if j < NB:
                    add_part(NB - 1, j)
                last_norms(j)

        @block.gpsimd
        def _(pool):
            def split_x(g, s):
                pool.wait_ge(x_hi_made, g + 1)
                pool.tensor_tensor(x_lo[:, s, :], x_in[:, s, :], x_hi[:, s, :], ALU.subtract).then_inc(x_lo_made, 1)

            def fold(g, s):
                at_least(pool, x0_lo_made, g - 1)
                step = g * FOLDS
                for c2 in range(HALF):
                    pool.wait_ge(prods_made, g * GROUPS + (c2 + 1) * QUARTERS)
                    left = K // 2
                    while left:
                        out = x0_acc[:, s, HALF + c2:HALF + c2 + 1, :] if left == 1 else prods[:, c2, 0:left, :]
                        if left < K // 2:
                            pool.wait_ge(fold_step, step)
                        pool.tensor_tensor(out, prods[:, c2, 0:left, :], prods[:, c2, left:2 * left, :],
                                           ALU.add).then_inc(fold_step, 1)
                        step = step + 1
                        left //= 2

            def split_x0(g, s):
                pool.wait_ge(x0_hi_made, g + 1)
                pool.tensor_tensor(x0_lo[:, bass.ds(g * CH, CH), :], x0_acc[:, s, :, :],
                                   x0_hi[:, bass.ds(g * CH, CH), :], ALU.subtract).then_inc(x0_lo_made, 1)

            def first_stage(pair, s):
                g = pair * 2 + s
                if not isinstance(pair, int) or g + 1 < NB:
                    split_x(g + 1, 1 - s)
                fold(g, s)
                if not isinstance(pair, int) or g > 0:
                    split_x0(g - 1, 1 - s)

            def split_adj(r, g):
                s = g % 2
                pool.wait_ge(adj_hi_made[s], lo_count(r, g))
                pool.tensor_tensor(adj_lo[:, s, :, :], row_in[:, g % RING, :, :], adj_hi[:, s, :, :],
                                   ALU.subtract).then_inc(adj_lo_made[s], 1)

            pool.wait_ge(w2_hi_made, 1)
            pool.tensor_tensor(W2_lo[:, :, :], W2_in, W2_hi[:, :, :], ALU.subtract).then_inc(w2_lo_made, 1)
            split_x(0, 0)
            for s in range(2):
                first_stage(0, s)
            with pool.Fori(1, NB // 2 - 1) as pair:
                for s in range(2):
                    first_stage(pair, s)
            for s in range(2):
                first_stage(NB // 2 - 1, s)
            split_x0(NB - 1, 1)
            for g in ACT_ROUNDS:
                split_adj(0, g)
            with pool.Fori(1, NB) as r:
                for g in range(NB):
                    split_adj(r, g)


def kernel(x, adj, L0_gnn_W1, L0_gnn_W2, L0_gnn_b, L1_gnn_W, L1_gnn_B):
    import numpy as np
    import concourse.bacc as bacc
    from concourse.bass_utils import run_bass_kernel_spmd

    x, adj, W1, W2, b0, W, B = (np.asarray(a) for a in (x, adj, L0_gnn_W1, L0_gnn_W2, L0_gnn_b, L1_gnn_W, L1_gnn_B))
    n, d = x.shape
    blocks = n // BW
    adjT = adj.reshape(blocks, BW, blocks, CH, P).transpose(0, 2, 4, 3, 1)
    arrays = {
        "adjT": adjT, "xT": x.T, "W1": W1, "W1T": W1.T, "W2": W2, "b0": b0, "W": W,
        "B": np.broadcast_to(B, (P, CH, d)),
    }
    arrays = {f"{name}_dram": np.ascontiguousarray(a) for name, a in arrays.items()}
    nc = bacc.Bacc("TRN2", target_bir_lowering=False, num_devices=1)
    args = [nc.dram_tensor(name, a.shape, mybir.dt.from_np(a.dtype), kind="ExternalInput").ap()
            for name, a in arrays.items()]
    outT = nc.dram_tensor("outT_dram", (d, n), F32, kind="ExternalOutput").ap()
    gnn_kernel(nc, *args, outT)
    result = run_bass_kernel_spmd(nc, [arrays], core_ids=[0])
    return np.ascontiguousarray(result.results[0]["outT_dram"].T)
```

```python
from contextlib import ExitStack

import concourse.bass as bass
from concourse import mybir

F32 = mybir.dt.float32
F32R = mybir.dt.float32r
ALU = mybir.AluOpType
ACT = mybir.ActivationFunctionType

P = 128
CH = 4
BW = CH * P
EPS = 1e-5
TINY = 2.0 ** -60
SCALE_STEP = 0
ACT_ROUNDS = (0, 4)
VECTOR_SPLITS = (0, 1, 2, 3, 4, 5, 6, 7, 8, 9, 11)
RING = 4
LAG = 3
LEAD = 1
SPLIT_LEAD = 3
ROW_LEAD = 5
COL_LEAD = 3
L1_BANKS = 4
EARLY = 7
HW_BANKS = (4, 2)
TAIL_LAG = 2
MEAN_LAG = 1
SQUARE_LAG = 2
SCALE_LAG = 3
OUT_LAG = 4
POOL_SQUARES = 5


def at_least(engine, semaphore, count):
    if not isinstance(count, int) or count > 0:
        engine.wait_ge(semaphore, count)


def block_of(tensor, index):
    return tensor[:, bass.ds(index * BW, BW)]


def gnn_kernel(nc, adjT, xT, W1, W1T, W2, b0, W, B, outT):
    NB = adjT.shape[0]
    K = W1.shape[1]
    D = xT.shape[0]
    N = NB * BW
    KG = CH
    QUARTERS = K // KG
    HALF = CH // 2
    GROUPS = HALF * QUARTERS
    STEPS = HALF * (K + 1)
    W2_HALF = [slice(h * K // 2, (h + 1) * K // 2) for h in range(2)]
    FOLDS = HALF * (K.bit_length() - 1)
    assert GROUPS % HW_BANKS[0] == 0 and GROUPS % HW_BANKS[1] == 0 and D == P and xT.shape[1] == N and NB % RING == 0 and NB % 2 == 0

    with ExitStack() as ctx:
        def sb(name, shape, dt=F32, stack=ctx):
            return stack.enter_context(nc.sbuf_tensor(name, shape, dt))

        def psum(name, shape, stack=ctx):
            return stack.enter_context(nc.psum_tensor(name, shape, F32))

        def sem(name):
            return ctx.enter_context(nc.semaphore(name))

        x0_hi = sb("x0_hi", [P, NB * CH, P], F32R)
        x0_lo = sb("x0_lo", [P, NB * CH, P], F32R)
        sumT = sb("sumT", [P, N])
        row_in = sb("row_in", [P, RING, CH, BW])
        col_in = sb("col_in", [P, RING, CH, BW])
        with ExitStack() as first:
            W2_in = sb("W2_in", [P, K, P], F32, first)
            sb("slot_1", [P, CH, BW], F32, first)
            row0_hi = sb("row0_hi", [P, CH, BW], F32R, first)
            row0_lo = sb("row0_lo", [P, CH, BW], F32R, first)
        wts = sb("wts", [P, RING, CH, BW])
        x_row = sb("x_row", [P, BW])
        W_sb = sb("W_sb", [P, P])
        W1_sb = sb("W1_sb", [P, K])
        W1T_sb = sb("W1T_sb", [K, P])
        b0_sb = sb("b0_sb", [K, P])
        W1b = sb("W1b", [P, P])
        B_sb = sb("B_sb", [P, CH, P])
        mean_w = sb("mean_w", [P, P])
        node = sb("node", [P, 2, CH, K])
        with ExitStack() as first:
            W2_hi = sb("W2_hi", [P, K, P], F32R, first)
            W2_lo = sb("W2_lo", [P, K, P], F32R, first)
            x_in = sb("x_in", [P, 2, BW], F32, first)
            x_hi = sb("x_hi", [P, 2, BW], F32R, first)
            x_lo = sb("x_lo", [P, 2, BW], F32R, first)
            x0_acc = sb("x0_acc", [P, 2, CH, P], F32, first)
            part_acc = sb("part_acc", [P, HALF, 2, P], F32, first)
            prods = sb("prods", [P, HALF, K, P], F32, first)
        adj_hi = sb("adj_hi", [P, 2, CH, BW], F32R)
        adj_lo = sb("adj_lo", [P, 2, CH, BW], F32R)
        y = sb("y", [P, BW])
        yc = sb("yc", [P, BW])
        sq = sb("sq", [P, BW])
        rstd = sb("rstd", [P, BW])
        x1T = sb("x1T", [P, BW])
        msg = sb("msg", [P, CH, P])
        sq_f = [row_in[:, s, 0, :] for s in range(RING)]
        rstd_f = [row_in[:, s, 1, :] for s in range(RING)]

        acc_ps = psum("acc_ps", [P, BW])
        mean_ps = psum("mean_ps", [P, BW])
        node_ps = [acc_ps[:, 0:CH * K], mean_ps[:, 0:CH * K]]
        w1b_ps = mean_ps[:, 0:P]
        with ExitStack() as first:
            hw_ps = [psum(f"hw_ps_{half}", [P, banks, KG, P], first) for half, banks in enumerate(HW_BANKS)]
        l1_ps = psum("l1_ps", [P, L1_BANKS, BW])
        var_ps = psum("var_ps", [P, BW])
        msg_ps = psum("msg_ps", [P, CH, P])
        mean_f = [mean_ps[:, :], msg_ps[:, :, :].rearrange("p c f -> p (c f)")]
        var_f = [var_ps[:, :], acc_ps[:, :]]

        const_in = sem("const_in")
        w1_in = sem("w1_in")
        w2_in = [sem(f"w2_in_{h}") for h in range(2)]
        x_in_sem = [sem(f"x_in_{s}") for s in range(2)]
        x_row_in = sem("x_row_in")
        row_tile_in = [sem(f"row_tile_in_{s}") for s in range(RING)]
        col_tile_in = [sem(f"col_tile_in_{s}") for s in range(RING)]
        mean_w_filled = sem("mean_w_filled")
        sum_cleared = sem("sum_cleared")
        w1b_made = sem("w1b_made")
        w1b_copied = sem("w1b_copied")
        w2_hi_made = sem("w2_hi_made")
        w2_lo_made = sem("w2_lo_made")
        x_hi_made = sem("x_hi_made")
        x_lo_made = sem("x_lo_made")
        node_made = sem("node_made")
        node_copied = sem("node_copied")
        hw_made = [sem(f"hw_made_{h}") for h in range(2)]
        prods_made = sem("prods_made")
        fold_step = sem("fold_step")
        sum_step = sem("sum_step")
        x0_hi_made = sem("x0_hi_made")
        x0_lo_made = sem("x0_lo_made")
        adj_hi_made = [sem(f"adj_hi_made_{s}") for s in range(2)]
        adj_lo_made = [sem(f"adj_lo_made_{s}") for s in range(2)]
        row_tile_done = sem("row_tile_done")
        acc_done = sem("acc_done")
        y_made = sem("y_made")
        mean_made = sem("mean_made")
        yc_made = sem("yc_made")
        sq_made = sem("sq_made")
        pool_sq_made = sem("pool_sq_made")
        var_made = sem("var_made")
        ln_var_made = sem("ln_var_made")
        rstd_made = sem("rstd_made")
        x1_made = sem("x1_made")
        x1_added = sem("x1_added")
        msg_made = sem("msg_made")
        msg_copied = sem("msg_copied")
        ln_made = sem("ln_made")
        inv_made = sem("inv_made")
        square_made = sem("square_made")
        exp_made = sem("exp_made")
        wts_made = sem("wts_made")
        col_tile_done = sem("col_tile_done")
        sum_added = sem("sum_added")
        out_made = sem("out_made")
        out_stored = sem("out_stored")

        CONSTS = 4 * 16

        def row_tile_count(r, g):
            return 16 * (NB // RING * r + g // RING + 1)

        def numbered(c, u):
            return NB * c + u, u % RING, u % NB, c + u // NB

        def parts(r, g):
            if is_row(r, 0) and g < NB:
                if g % 3 == 2:
                    return row0_hi[:, :, :], row0_lo[:, :, :]
                return adj_hi[:, g % 3, :, :], adj_lo[:, g % 3, :, :]
            return adj_hi[:, g % 2, :, :], adj_lo[:, g % 2, :, :]

        def parts_used(r, g):
            return NB * r + g - (2 if is_row(r, 0) and g < NB else 1)

        def by_scalar(r, g):
            return is_row(r, 0) and g < NB or g % NB in ACT_ROUNDS

        def is_row(r, number):
            return isinstance(r, int) and r == number

        def message_step(r):
            return 1 if is_row(r, 1) else LAG - 1

        def exists(r, g):
            return not isinstance(r, int) or 0 <= NB * r + g < NB * NB

        def is_early(c, u):
            return isinstance(c, int) and NB * c + u < NB + LEAD - EARLY

        def tail_tiles(g):
            if g == LAG - 2:
                return list(range(g - LAG, g - TAIL_LAG + 1))
            return [g - (LAG if g < LAG - 2 else TAIL_LAG)]

        def dve_steps(n):
            return KG * (n + 1) + (n + 1) // QUARTERS

        def lo_count(r, g):
            return NB // 2 * r + g // 2 + 1

        block = ctx.enter_context(nc.Block())

        @block.sync
        def _(sp):
            def load_row_tile(r, g):
                at_least(sp, adj_lo_made[g % 2], lo_count(r, g - RING))
                sp.dma_start(row_in[:, g % RING, :, :], adjT[r + g // NB, g % NB]).then_inc(row_tile_in[g % RING], 16)

            def load_col_tile(c, u):
                t, slot, j, col = numbered(c, u)
                at_least(sp, wts_made, t - RING + 1)
                sp.dma_start(col_in[:, slot, :, :], adjT[j, col]).then_inc(col_tile_in[slot], 16)

            def load_x_row(r):
                at_least(sp, y_made, r)
                sp.dma_start(x_row[:, :], block_of(xT, r)).then_inc(x_row_in, 16)

            def load_x(pair, s):
                g = pair * 2 + s
                at_least(sp, x_lo_made, g - 1)
                at_least(sp, node_made, g - 1)
                sp.dma_start(x_in[:, s, :], block_of(xT, g)).then_inc(x_in_sem[s], 16)

            def load_W2(h):
                sp.dma_start(W2_in[:, W2_HALF[h], :], W2[W2_HALF[h]].rearrange("k c f -> c k f")).then_inc(w2_in[h], 16)

            load_W2(0)
            load_x(0, 0)
            sp.dma_start(W1_sb[:, :], W1).then_inc(w1_in, 16)
            load_W2(1)
            load_x(0, 1)
            sp.dma_start(W1T_sb[:, :], W1T).then_inc(const_in, 16)
            sp.dma_start(b0_sb[:, :], b0).then_inc(const_in, 16)
            sp.dma_start(W_sb[:, :], W).then_inc(const_in, 16)
            sp.dma_start(B_sb[:, :, :], B).then_inc(const_in, 16)
            load_x_row(0)
            for s in range(2):
                load_x(1, s)
            for g in range(RING):
                load_row_tile(0, g)
                load_col_tile(0, g)
            with sp.Fori(2, NB // 2) as pair:
                for s in range(2):
                    load_x(pair, s)
            for g in range(RING, ROW_LEAD):
                load_row_tile(0, g)

            def loads(r):
                if not isinstance(r, int) or 0 < r < NB:
                    load_x_row(r)
                for g in range(NB):
                    if exists(r, g + ROW_LEAD):
                        load_row_tile(r, g + ROW_LEAD)
                    if exists(r - 1, g + COL_LEAD) and not (is_row(r, 0) or is_row(r, 1) and g + COL_LEAD < RING):
                        load_col_tile(r - 1, g + COL_LEAD)

            for r in (0, 1):
                loads(r)
            with sp.Fori(2, NB - 1) as r:
                loads(r)
            for r in (NB - 1, NB):
                loads(r)
            for j in range(NB):
                sp.wait_ge(out_made, j + 1)
                sp.dma_start(block_of(outT, j), block_of(sumT, j)).then_inc(out_stored, 16)
            sp.wait_ge(out_stored, 16 * NB)

        @block.tensor
        def _(pe):
            def node_product(pair, s):
                g = pair * 2 + s
                pe.wait_ge(x_in_sem[s], 16 * (pair + 1))
                at_least(pe, node_copied, g - 1)
                for c in range(CH):
                    mm = pe.matmul(node_ps[s][:, c * K:(c + 1) * K], x_in[:, s, c * P:(c + 1) * P], W1_sb[:, :],
                                   start=True, stop=True)
                mm.then_inc(node_made, 1)

            def hidden(pair, s):
                g = pair * 2 + s
                pe.wait_ge(x_lo_made, g + 1)
                for n in range(GROUPS):
                    for half in range(2):
                        c = HALF * half + n // QUARTERS
                        q = n % QUARTERS
                        banks = HW_BANKS[half]
                        if half == 0:
                            at_least(pe, sum_step, (g - int(n < banks)) * STEPS + dve_steps((n - banks) % GROUPS))
                        else:
                            at_least(pe, prods_made, g * GROUPS + n + 1 - banks)
                        if is_row(pair, 0) and s == 0 and half == 0 and n in (0, QUARTERS // 2):
                            pe.wait_ge(w2_lo_made, 1 + n // (QUARTERS // 2))
                        out = hw_ps[half][:, n % banks, :, :]
                        nodes = slice(c * P, (c + 1) * P)
                        ks = slice(q * KG, (q + 1) * KG)
                        pe.matmul(out, x_hi[:, s, nodes], W2_hi[:, ks, :], start=True, stop=False)
                        pe.matmul(out, x_hi[:, s, nodes], W2_lo[:, ks, :], start=False, stop=False)
                        pe.matmul(out, x_lo[:, s, nodes], W2_hi[:, ks, :], start=False,
                                  stop=True).then_inc(hw_made[half], 1)

            def first_stage(pair, s):
                if not isinstance(pair, int) or pair * 2 + s + 1 < NB:
                    node_product(pair + s, 1 - s)
                hidden(pair, s)

            def row_tile(r, g):
                if g == 0:
                    at_least(pe, y_made, r)
                if is_row(r, 0):
                    pe.wait_ge(x0_lo_made, g + 1)
                pe.wait_ge(adj_lo_made[g % 2], lo_count(r, g))
                hi, lo = parts(r, g)
                for c in range(CH):
                    k = g * CH + c
                    pe.matmul(acc_ps[:, :], x0_hi[:, k, :], hi[:, c, :], start=(g == 0 and c == 0), stop=False)
                    pe.matmul(acc_ps[:, :], x0_lo[:, k, :], hi[:, c, :], start=False, stop=False)
                    mm = pe.matmul(acc_ps[:, :], x0_hi[:, k, :], lo[:, c, :], start=False, stop=False)
                mm.then_inc(row_tile_done, 1)

            def node_bias(r):
                pe.wait_ge(x_row_in, 16 * (r + 1))
                if is_row(r, 0):
                    pe.wait_ge(w1b_copied, 1)
                pe.matmul(acc_ps[:, :], W1b[:, :], x_row[:, :], start=False, stop=True).then_inc(acc_done, 1)

            def mean(r):
                pe.wait_ge(y_made, r + 1)
                pe.matmul(mean_ps[:, :], mean_w[:, :], y[:, :], start=True, stop=True).then_inc(mean_made, 1)

            def variance(r):
                pe.wait_ge(sq_made, r + 1)
                pe.matmul(var_ps[:, :], mean_w[:, :], sq[:, :], start=True, stop=True).then_inc(var_made, 1)

            def messages(r):
                pe.wait_ge(x1_made, r + 1)
                for c in range(CH):
                    mm = pe.matmul(msg_ps[:, c, :], x1T[:, c * P:(c + 1) * P], W_sb[:, :], start=True, stop=True)
                mm.then_inc(msg_made, 1)

            def col_tile(c, u):
                t, slot, j, col = numbered(c, u)
                if j == 0:
                    pe.wait_ge(msg_copied, col + 1)
                at_least(pe, sum_added, t - L1_BANKS + 1)
                pe.wait_ge(wts_made, t + 1)
                for k in range(CH):
                    mm = pe.matmul(l1_ps[:, j % L1_BANKS, :], msg[:, k, :], wts[:, slot, k, :],
                                   start=(k == 0), stop=(k == CH - 1))
                mm.then_inc(col_tile_done, 1)

            def row(r):
                before = not isinstance(r, int) or r > 0
                for g in range(NB):
                    if before and not is_row(r, 1) and g == message_step(r):
                        messages(r - 1)
                    row_tile(r, g)
                    if is_row(r, 1) and g == message_step(r):
                        messages(r - 1)
                    if g == NB - 1:
                        node_bias(r)
                    if exists(r - 1, g - LAG):
                        col_tile(r - 1, g - LAG)
                    if before and g == 0:
                        variance(r - 1)
                    if g == NB - 1:
                        mean(r)

            def tail(g):
                if g == LAG - 1:
                    messages(NB - 1)
                for u in tail_tiles(g):
                    if u < NB:
                        col_tile(NB - 1, u)
                if g == 0:
                    variance(NB - 1)
                i = g - TAIL_LAG - MEAN_LAG
                if 0 <= i < NB:
                    pe.wait_ge(sum_added, NB * (NB - 1) + i + 1)
                    pe.matmul(mean_f[i % 2], mean_w[:, :], block_of(sumT, i),
                              start=True, stop=True).then_inc(mean_made, 1)
                i = g - TAIL_LAG - SCALE_LAG
                if 0 <= i < NB:
                    if i >= 2:
                        pe.wait_ge(rstd_made, NB + i - 1)
                    if i < POOL_SQUARES:
                        pe.wait_ge(pool_sq_made, i + 1)
                    else:
                        pe.wait_ge(sq_made, NB + i - POOL_SQUARES + 1)
                    pe.matmul(var_f[i % 2], mean_w[:, :], sq_f[i % RING],
                              start=True, stop=True).then_inc(var_made, 1)

            pe.wait_ge(w1_in, 16)
            node_product(0, 0)
            for s in range(2):
                first_stage(0, s)
            with pe.Fori(1, NB // 2 - 1) as pair:
                for s in range(2):
                    first_stage(pair, s)
            for s in range(2):
                first_stage(NB // 2 - 1, s)

            pe.wait_ge(const_in, CONSTS)
            pe.wait_ge(node_copied, NB)
            pe.matmul(w1b_ps, W1T_sb[:, :], b0_sb[:, :], start=True, stop=True).then_inc(w1b_made, 1)
            pe.wait_ge(mean_w_filled, 1)
            for r in (0, 1):
                row(r)
            with pe.Fori(2, NB - 1) as r:
                row(r)
            row(NB - 1)
            for g in range(NB + TAIL_LAG + SCALE_LAG):
                tail(g)

        @block.scalar
        def _(act):
            def copy_node(g, s):
                act.wait_ge(node_made, g + 1)
                at_least(act, sum_step, (g - 1) * STEPS)
                at_least(act, prods_made, (g - 1) * GROUPS)
                act.activation(node[:, s, :, :], node_ps[s].rearrange("p (c k) -> p c k", k=K),
                               ACT.Copy).then_inc(node_copied, 1)

            def first_stage(pair, s):
                g = pair * 2 + s
                if not isinstance(pair, int) or g + 1 < NB:
                    copy_node(g + 1, 1 - s)
                act.wait_ge(node_copied, g + 1)
                for n in range(GROUPS):
                    c2, q = n // QUARTERS, n % QUARTERS
                    act.wait_ge(hw_made[1], g * GROUPS + n + 1)
                    if q == 0:
                        at_least(act, fold_step, (g - 1) * FOLDS + (c2 + 1) * FOLDS // HALF)
                    for kk in range(KG):
                        k = q * KG + kk
                        op = act.activation(prods[:, c2, k, :], hw_ps[1][:, n % HW_BANKS[1], kk, :], ACT.Copy,
                                            scale=node[:, s, HALF + c2, k:k + 1])
                    op.then_inc(prods_made, 1)

            def take_ln(c, u):
                t, slot, _, _ = numbered(c, u)
                act.wait_ge(col_tile_in[slot], 16 * (NB // RING * c + u // RING + 1))
                at_least(act, col_tile_done, t - RING + 1)
                if isinstance(c, int) and c == 0 and u in (2, 3):
                    act.wait_ge(row_tile_done, 6)
                act.activation(wts[:, slot, :, :], col_in[:, slot, :, :], ACT.Ln, bias=TINY).then_inc(ln_made, 1)

            def take_inverse(c, u):
                t, slot, _, _ = numbered(c, u)
                act.wait_ge(ln_made, t + 1)
                act.activation(wts[:, slot, :, :], wts[:, slot, :, :], ACT.Exp, scale=-1.0).then_inc(inv_made, 1)

            def take_exp(c, u):
                t, slot, _, _ = numbered(c, u)
                act.wait_ge(square_made, t + 1)
                act.activation(wts[:, slot, :, :], wts[:, slot, :, :], ACT.Exp, bias=-2.0,
                               scale=-2.0).then_inc(exp_made, 1)

            def round_adj(r, g):
                act.wait_ge(row_tile_in[g % RING], row_tile_count(r, g))
                at_least(act, row_tile_done, parts_used(r, g))
                act.activation(parts(r, g)[0], row_in[:, g % RING, :, :],
                               ACT.Copy).then_inc(adj_hi_made[g % 2], 1)

            def square(n, into, centred):
                act.wait_ge(yc_made, n + 1)
                act.activation(into, centred, ACT.Square).then_inc(sq_made, 1)

            def inverse_root(n, into, variance):
                act.wait_ge(var_made, n + 1)
                act.activation(into, variance, ACT.Ln, bias=EPS).then_inc(ln_var_made, 1)
                act.wait_ge(ln_var_made, n + 1)
                act.activation(into, into, ACT.Exp, scale=-0.5).then_inc(rstd_made, 1)

            act.preload_act_table_set("natural_log_exp_and_others")
            copy_node(0, 0)
            for s in range(2):
                first_stage(0, s)
            with act.Fori(1, NB // 2 - 1) as pair:
                for s in range(2):
                    first_stage(pair, s)
            for s in range(2):
                first_stage(NB // 2 - 1, s)

            for half in range(2):
                act.wait_ge(hw_made[half], NB * GROUPS)
            for g in range(SPLIT_LEAD):
                round_adj(0, g)

            def row(r):
                before = not isinstance(r, int) or r > 0
                for g in range(NB):
                    c, u = (r - 1, g + LEAD) if before else (0, g + LEAD - EARLY)
                    starts = exists(c, u) and not (before and is_early(c, u))
                    rounds = exists(r, g + SPLIT_LEAD) and by_scalar(r, g + SPLIT_LEAD)
                    if is_row(r, 0) and g == NB - 1:
                        square(r, sq[:, :], yc[:, :])
                    if is_row(r, 0) and rounds:
                        round_adj(r, g + SPLIT_LEAD)
                    if starts:
                        take_ln(c, u)
                    if before and not is_row(r, 1) and g == 0:
                        inverse_root(r - 1, rstd[:, :], var_ps[:, :])
                    if starts:
                        take_inverse(c, u)
                    if is_row(r, 0) and g == NB - 1:
                        inverse_root(r, rstd[:, :], var_ps[:, :])
                    if not is_row(r, 0) and g == NB - 1:
                        square(r, sq[:, :], yc[:, :])
                    if exists(c, u - 1) and not (before and is_early(c, u)):
                        take_exp(c, u - 1)
                    if rounds and not is_row(r, 0):
                        round_adj(r, g + SPLIT_LEAD)

            def tail(g):
                u = g + LEAD
                if u < NB:
                    take_ln(NB - 1, u)
                if g == 0:
                    inverse_root(NB - 1, rstd[:, :], var_ps[:, :])
                if u < NB:
                    take_inverse(NB - 1, u)
                if u - 1 < NB:
                    take_exp(NB - 1, u - 1)
                i = g - TAIL_LAG - SQUARE_LAG
                if POOL_SQUARES <= i < NB:
                    square(NB + i, sq_f[i % RING], block_of(sumT, i))
                i = g - TAIL_LAG - SCALE_LAG
                if 0 <= i < NB:
                    at_least(act, out_made, i + 1 - RING)
                    inverse_root(NB + i, rstd_f[i % RING], var_f[i % 2])

            for r in (0, 1):
                row(r)
            with act.Fori(2, NB - 1) as r:
                row(r)
            row(NB - 1)
            for g in range(NB + TAIL_LAG + SCALE_LAG):
                tail(g)

        @block.vector
        def _(dve):
            def round_x(pair, s):
                g = pair * 2 + s
                dve.wait_ge(x_in_sem[s], 16 * (pair + 1))
                for half in range(2):
                    at_least(dve, hw_made[half], (g - 1) * GROUPS)
                dve.tensor_copy(x_hi[:, s, :], x_in[:, s, :]).then_inc(x_hi_made, 1)
                dve.wait_ge(x_hi_made, g + 1)
                dve.tensor_tensor(x_lo[:, s, :], x_in[:, s, :], x_hi[:, s, :], ALU.subtract).then_inc(x_lo_made, 1)

            def sum_over_k(g, s):
                dve.wait_ge(node_copied, g + 1)
                at_least(dve, x0_lo_made, g - 1)
                for n in range(GROUPS):
                    c, q = n // QUARTERS, n % QUARTERS
                    dve.wait_ge(hw_made[0], g * GROUPS + n + 1)
                    for kk in range(KG):
                        k = q * KG + kk
                        acc = part_acc[:, c, k % 2, :]
                        hw = hw_ps[0][:, n % HW_BANKS[0], kk, :]
                        scale = node[:, s, c, k:k + 1]
                        step = g * STEPS + c * (K + 1) + k
                        if k < 2:
                            dve.tensor_scalar(acc, hw, scale, None, ALU.mult).then_inc(sum_step, 1)
                        else:
                            dve.wait_ge(sum_step, step - 1)
                            dve.scalar_tensor_tensor(out=acc, in0=hw, scalar=scale, in1=acc, op0=ALU.mult,
                                                     op1=ALU.add).then_inc(sum_step, 1)
                    if q == QUARTERS - 1:
                        dve.wait_ge(sum_step, g * STEPS + c * (K + 1) + K)
                        dve.tensor_tensor(x0_acc[:, s, c, :], part_acc[:, c, 0, :], part_acc[:, c, 1, :],
                                          ALU.add).then_inc(sum_step, 1)

            def round_x0(g, s):
                dve.wait_ge(sum_step, (g + 1) * STEPS)
                dve.wait_ge(fold_step, (g + 1) * FOLDS)
                dve.tensor_copy(x0_hi[:, bass.ds(g * CH, CH), :], x0_acc[:, s, :, :]).then_inc(x0_hi_made, 1)
                dve.wait_ge(x0_hi_made, g + 1)
                dve.tensor_tensor(x0_lo[:, bass.ds(g * CH, CH), :], x0_acc[:, s, :, :],
                                  x0_hi[:, bass.ds(g * CH, CH), :], ALU.subtract).then_inc(x0_lo_made, 1)

            def first_stage(pair, s):
                g = pair * 2 + s
                if not isinstance(pair, int) or g + 1 < NB:
                    round_x(pair + s, 1 - s)
                sum_over_k(g, s)
                if not isinstance(pair, int) or g > 0:
                    round_x0(g - 1, 1 - s)

            def mask(c, u):
                t, slot, _, _ = numbered(c, u)
                dve.wait_ge(exp_made, t + 1)
                dve.scalar_tensor_tensor(out=wts[:, slot, :, :].rearrange("p c n -> p (c n)"),
                                         in0=col_in[:, slot, :, :].rearrange("p c n -> p (c n)"), scalar=1.0,
                                         in1=wts[:, slot, :, :].rearrange("p c n -> p (c n)"), op0=ALU.is_lt,
                                         op1=ALU.mult).then_inc(wts_made, 1)

            def take_square(c, u):
                t, slot, _, _ = numbered(c, u)
                dve.wait_ge(inv_made, t + 1)
                w = wts[:, slot, :, :].rearrange("p c n -> p (c n)")
                dve.scalar_tensor_tensor(out=w, in0=w, scalar=2.0, in1=w, op0=ALU.subtract,
                                         op1=ALU.mult).then_inc(square_made, 1)

            def round_adj(r, g):
                dve.wait_ge(row_tile_in[g % RING], row_tile_count(r, g))
                at_least(dve, row_tile_done, parts_used(r, g))
                dve.tensor_copy(parts(r, g)[0], row_in[:, g % RING, :, :]).then_inc(adj_hi_made[g % 2], 1)

            def split_adj(r, g):
                dve.wait_ge(adj_hi_made[g % 2], lo_count(r, g))
                hi, lo = parts(r, g)
                dve.tensor_tensor(lo, row_in[:, g % RING, :, :], hi, ALU.subtract).then_inc(adj_lo_made[g % 2], 1)

            def residual(r):
                dve.wait_ge(acc_done, r + 1)
                dve.scalar_tensor_tensor(out=y[:, :], in0=acc_ps[:, :], scalar=0.0, in1=x_row[:, :], op0=ALU.max,
                                         op1=ALU.add).then_inc(y_made, 1)

            def centre(r):
                dve.wait_ge(mean_made, r + 1)
                dve.tensor_tensor(yc[:, :], y[:, :], mean_ps[:, :], ALU.subtract).then_inc(yc_made, 1)

            def scale_row(r):
                dve.wait_ge(rstd_made, r + 1)
                dve.tensor_tensor(x1T[:, :], yc[:, :], rstd[:, :], ALU.mult).then_inc(x1_made, 1)
                dve.wait_ge(x1_made, r + 1)
                if is_row(r, 0):
                    dve.wait_ge(sum_cleared, 1)
                at_least(dve, sum_added, r * NB + SCALE_STEP - LAG + 1)
                dve.tensor_tensor(block_of(sumT, r), block_of(sumT, r), x1T[:, :], ALU.add).then_inc(x1_added, 1)

            def copy_messages(r):
                dve.wait_ge(msg_made, r + 1)
                dve.tensor_tensor(msg[:, :, :], msg_ps[:, :, :], B_sb[:, :, :], ALU.add).then_inc(msg_copied, 1)

            def add_part(c, u):
                t, _, j, col = numbered(c, u)
                dve.wait_ge(col_tile_done, t + 1)
                if isinstance(c, int) and c == 0 and u == 0:
                    dve.wait_ge(sum_cleared, 1)
                at_least(dve, x1_added, c + int(u + LAG > SCALE_STEP))
                at_least(dve, sum_added, col * NB)
                dve.tensor_tensor(block_of(sumT, j), l1_ps[:, j % L1_BANKS, :], block_of(sumT, j),
                                  ALU.add).then_inc(sum_added, 1)

            def split_W2(h):
                ks = W2_HALF[h]
                dve.wait_ge(w2_in[h], 16)
                dve.tensor_copy(W2_hi[:, ks, :], W2_in[:, ks, :]).then_inc(w2_hi_made, 1)
                dve.wait_ge(w2_hi_made, h + 1)
                dve.tensor_tensor(W2_lo[:, ks, :], W2_in[:, ks, :], W2_hi[:, ks, :],
                                  ALU.subtract).then_inc(w2_lo_made, 1)

            split_W2(0)
            round_x(0, 0)
            split_W2(1)
            for s in range(2):
                first_stage(0, s)
            with dve.Fori(1, NB // 2 - 1) as pair:
                for s in range(2):
                    first_stage(pair, s)
            for s in range(2):
                first_stage(NB // 2 - 1, s)

            for half in range(2):
                dve.wait_ge(hw_made[half], NB * GROUPS)
            split_adj(0, 0)
            round_x0(NB - 1, 1)
            dve.wait_ge(x0_lo_made, NB)
            split_adj(0, 1)
            split_adj(0, 2)
            dve.wait_ge(w1b_made, 1)
            dve.tensor_copy(W1b[:, :], w1b_ps).then_inc(w1b_copied, 1)

            def row(r):
                before = not isinstance(r, int) or r > 0
                for g in range(NB):
                    c, u = (r - 1, g + LEAD) if before else (0, g + LEAD - EARLY)
                    if is_row(r, 0) and g == NB - 2:
                        residual(r)
                    if exists(r - 1, g - LAG):
                        add_part(r - 1, g - LAG)
                    if before and g == message_step(r):
                        copy_messages(r - 1)
                    if exists(c, u - 2) and not (before and is_early(c, u)):
                        mask(c, u - 2)
                    if g == NB - 1 and not is_row(r, 0):
                        centre(r)
                    if exists(r, g + SPLIT_LEAD) and not by_scalar(r, g + SPLIT_LEAD):
                        round_adj(r, g + SPLIT_LEAD)
                    if isinstance(r, int) and NB * r + g + SPLIT_LEAD in VECTOR_SPLITS:
                        split_adj(r, g + SPLIT_LEAD)
                    if g == NB - 2 and not is_row(r, 0):
                        residual(r)
                    if g == NB - 2 and is_row(r, 0):
                        centre(r)
                    if before and not is_row(r, 1) and g == SCALE_STEP:
                        scale_row(r - 1)
                    if exists(c, u) and not (before and is_early(c, u)):
                        take_square(c, u)
                    if is_row(r, 0) and g == NB - 1:
                        scale_row(r)

            def tail(g):
                def add_parts():
                    for u in tail_tiles(g):
                        if u < NB:
                            add_part(NB - 1, u)

                u = g + LEAD
                if u - 2 < NB:
                    mask(NB - 1, u - 2)
                i = g - TAIL_LAG - SQUARE_LAG
                if 0 <= i < NB:
                    dve.wait_ge(mean_made, NB + i + 1)
                    dve.tensor_tensor(block_of(sumT, i), block_of(sumT, i), mean_f[i % 2],
                                      ALU.subtract).then_inc(yc_made, 1)
                i = g - TAIL_LAG - OUT_LAG
                if 0 <= i < NB:
                    dve.wait_ge(rstd_made, NB + i + 1)
                    dve.tensor_tensor(block_of(sumT, i), block_of(sumT, i), rstd_f[i % RING],
                                      ALU.mult).then_inc(out_made, 1)
                if g < TAIL_LAG:
                    add_parts()
                if g == SCALE_STEP:
                    scale_row(NB - 1)
                if g == TAIL_LAG - 1:
                    copy_messages(NB - 1)
                if u < NB:
                    take_square(NB - 1, u)
                if g >= TAIL_LAG:
                    add_parts()

            for r in (0, 1):
                row(r)
            with dve.Fori(2, NB - 1) as r:
                row(r)
            row(NB - 1)
            for g in range(NB + TAIL_LAG + OUT_LAG):
                tail(g)

        @block.gpsimd
        def _(pool):
            def fold(g, s):
                at_least(pool, x0_lo_made, g - 1)
                step = g * FOLDS
                for c2 in range(HALF):
                    pool.wait_ge(prods_made, g * GROUPS + (c2 + 1) * QUARTERS)
                    left = K // 2
                    while left:
                        out = x0_acc[:, s, HALF + c2:HALF + c2 + 1, :] if left == 1 else prods[:, c2, 0:left, :]
                        if left < K // 2:
                            pool.wait_ge(fold_step, step)
                        pool.tensor_tensor(out, prods[:, c2, 0:left, :], prods[:, c2, left:2 * left, :],
                                           ALU.add).then_inc(fold_step, 1)
                        step = step + 1
                        left //= 2

            def first_stage(pair, s):
                g = pair * 2 + s
                fold(g, s)

            def split_adj(r, g):
                s = g % 2
                pool.wait_ge(adj_hi_made[s], lo_count(r, g))
                pool.tensor_tensor(adj_lo[:, s, :, :], row_in[:, g % RING, :, :], adj_hi[:, s, :, :],
                                   ALU.subtract).then_inc(adj_lo_made[s], 1)

            pool.memset(mean_w[:, :], 1.0 / D).then_inc(mean_w_filled, 1)
            pool.memset(sumT[:, :], 0.0).then_inc(sum_cleared, 1)
            for s in range(2):
                first_stage(0, s)
            with pool.Fori(1, NB // 2 - 1) as pair:
                for s in range(2):
                    first_stage(pair, s)
            for s in range(2):
                first_stage(NB // 2 - 1, s)
            for g in range(NB):
                if NB + g not in VECTOR_SPLITS:
                    split_adj(1, g)
            with pool.Fori(2, NB) as r:
                for g in range(NB):
                    split_adj(r, g)

            for i in range(POOL_SQUARES):
                pool.wait_ge(yc_made, NB + i + 1)
                pool.tensor_tensor(sq_f[i % RING], block_of(sumT, i), block_of(sumT, i),
                                   ALU.mult).then_inc(pool_sq_made, 1)


def kernel(x, adj, L0_gnn_W1, L0_gnn_W2, L0_gnn_b, L1_gnn_W, L1_gnn_B):
    import numpy as np
    import concourse.bacc as bacc
    from concourse.bass_utils import run_bass_kernel_spmd

    x, adj, W1, W2, b0, W, B = (np.asarray(a) for a in (x, adj, L0_gnn_W1, L0_gnn_W2, L0_gnn_b, L1_gnn_W, L1_gnn_B))
    n, d = x.shape
    blocks = n // BW
    adjT = adj.reshape(blocks, BW, blocks, CH, P).transpose(0, 2, 4, 3, 1)
    arrays = {
        "adjT": adjT, "xT": x.T, "W1": W1, "W1T": W1.T, "W2": W2, "b0": b0, "W": W,
        "B": np.broadcast_to(B, (P, CH, d)),
    }
    arrays = {f"{name}_dram": np.ascontiguousarray(a) for name, a in arrays.items()}
    nc = bacc.Bacc("TRN2", target_bir_lowering=False, num_devices=1)
    args = [nc.dram_tensor(name, a.shape, mybir.dt.from_np(a.dtype), kind="ExternalInput").ap()
            for name, a in arrays.items()]
    outT = nc.dram_tensor("outT_dram", (d, n), F32, kind="ExternalOutput").ap()
    gnn_kernel(nc, *args, outT)
    result = run_bass_kernel_spmd(nc, [arrays], core_ids=[0])
    return np.ascontiguousarray(result.results[0]["outT_dram"].T)
```
